# Optimizing a Trainium2 kernel written in Bass

```python
import numpy as np
import jax
import jax.numpy as jnp

def _softmax(x, axis=-1):
    return jax.nn.softmax(x, axis=axis)

def _gelu(x):
    return jax.nn.gelu(x, approximate=True)

def _silu(x):
    return jax.nn.silu(x)

def _sigmoid(x):
    return jax.nn.sigmoid(x)

def _layernorm(x, axis=-1, eps=1e-05):
    m = jnp.mean(x, axis=axis, keepdims=True)
    v = jnp.var(x, axis=axis, keepdims=True)
    return (x - m) / jnp.sqrt(v + eps)

def _scatter_add(tgt, idx, src, axis=0):
    return tgt.at[idx].add(src)

def _segment_sum(src, seg, n):
    return jax.ops.segment_sum(src, seg, n)
kernel_name = 'mk_adj_preln_d2_adj_r2_789519'

def setup_inputs(seed: int=0):
    np.random.seed(seed)
    _w = jnp.asarray

    def _rec_inputs():
        import jax
        import jax.numpy as jnp
        _gk = jax.random.key(seed)
        x = 7.22e-05 + 1 * jax.random.normal(jax.random.fold_in(_gk, 1), (16, 512, 256), jnp.float32)
        _a = jax.random.bernoulli(jax.random.fold_in(_gk, 2), 0.00390625, (512, 512))
        _a = jnp.logical_or(_a, jnp.swapaxes(_a, -1, -2))
        _a = jnp.logical_or(_a, jnp.eye(512, dtype=bool))
        adj = _a.astype(jnp.int32)
        return (x, adj)
    x, adj = _rec_inputs()

    def _L0_gnn_setup():
        import jax, jax.numpy as jnp
        import numpy as np
        LEAKY_ALPHA = 0.01
        NEG_INF = -1000000000.0
        LN_EPS = 1e-05

        def _gat_heads(x, adj, W, a):
            O = W.shape[-1]
            Wh = jnp.einsum('bnf,hfo->bhno', x, W)
            f1 = jnp.einsum('bhno,ho->bhn', Wh, a[:, :O])
            f2 = jnp.einsum('bhno,ho->bhn', Wh, a[:, O:])
            e = f1[:, :, :, None] + f2[:, :, None, :]
            e = jnp.where(e > 0, e, LEAKY_ALPHA * e)
            e = jnp.where(adj[None, None] > 0, e, NEG_INF)
            attn = jax.nn.softmax(e, axis=-1)
            return jnp.einsum('bhnm,bhmo->bhno', attn, Wh)
        key = jax.random.key(seed)
        ks = jax.random.split(key, 10)
        B, N, F_in, F_hid, H, F_out, D_ff = (8, 1024, 256, 256, 4, 256, 256)
        s = 0.05
        return {'enc_inputs': jax.random.normal(ks[0], (B, N, F_in), jnp.float32), 'adj': jax.random.randint(ks[1], (N, N), 0, 2, jnp.int32), 'W_heads': jax.random.normal(ks[2], (H, F_in, F_hid), jnp.float32) * s, 'a_heads': jax.random.normal(ks[3], (H, 2 * F_hid), jnp.float32) * s, 'W_out': jax.random.normal(ks[4], (H * F_hid, F_out), jnp.float32) * s, 'a_out': jax.random.normal(ks[5], (2 * F_out,), jnp.float32) * s, 'w1': jax.random.normal(ks[6], (F_out, D_ff), jnp.float32) * s, 'b1': jnp.zeros((D_ff,), jnp.float32), 'w2': jax.random.normal(ks[7], (D_ff, F_out), jnp.float32) * s, 'b2': jnp.zeros((F_out,), jnp.float32), 'ln_gamma': jnp.ones((F_out,), jnp.float32), 'ln_beta': jnp.zeros((F_out,), jnp.float32)}
    _L0_gnn_all = _L0_gnn_setup()
    _L0_gnn_in = {k: v for k, v in _L0_gnn_all.items() if k in ('W_heads', 'a_heads', 'W_out', 'a_out', 'w1', 'b1', 'w2', 'b2', 'ln_gamma', 'ln_beta')}
    del _L0_gnn_all

    def _L1_gnn_setup():
        import jax, jax.numpy as jnp
        import numpy as np
        B, K, DIN, DOUT = (32, 64, 256, 256)
        key = jax.random.key(seed)
        k1, k2, k3, k4 = jax.random.split(key, 4)
        x = jax.random.normal(k1, (B, K, DIN), dtype=jnp.float32)
        adj = jax.random.randint(k2, (K, K), 0, 2, dtype=jnp.int32)
        W = jax.random.normal(k3, (DOUT, 2 * DIN), dtype=jnp.float32) * 0.02
        b = jax.random.normal(k4, (DOUT,), dtype=jnp.float32) * 0.02
        return {'x': x, 'adj': adj, 'W': W, 'b': b}
    _L1_gnn_all = _L1_gnn_setup()
    _L1_gnn_in = {k: v for k, v in _L1_gnn_all.items() if k in ('W', 'b')}
    del _L1_gnn_all
    return {'x': x, 'adj': adj, 'L0_gnn_W_heads': _L0_gnn_in['W_heads'], 'L0_gnn_a_heads': _L0_gnn_in['a_heads'], 'L0_gnn_W_out': _L0_gnn_in['W_out'], 'L0_gnn_a_out': _L0_gnn_in['a_out'], 'L0_gnn_w1': _L0_gnn_in['w1'], 'L0_gnn_b1': _L0_gnn_in['b1'], 'L0_gnn_w2': _L0_gnn_in['w2'], 'L0_gnn_b2': _L0_gnn_in['b2'], 'L0_gnn_ln_gamma': _L0_gnn_in['ln_gamma'], 'L0_gnn_ln_beta': _L0_gnn_in['ln_beta'], 'L1_gnn_W': _L1_gnn_in['W'], 'L1_gnn_b': _L1_gnn_in['b']}

def reference(x, adj, L0_gnn_W_heads, L0_gnn_a_heads, L0_gnn_W_out, L0_gnn_a_out, L0_gnn_w1, L0_gnn_b1, L0_gnn_w2, L0_gnn_b2, L0_gnn_ln_gamma, L0_gnn_ln_beta, L1_gnn_W, L1_gnn_b):
    import jax
    import jax.numpy as jnp

    def _L0_gnn_ref(enc_inputs, adj, W_heads, a_heads, W_out, a_out, w1, b1, w2, b2, ln_gamma, ln_beta):
        import jax, jax.numpy as jnp
        import numpy as np
        LEAKY_ALPHA = 0.01
        NEG_INF = -1000000000.0
        LN_EPS = 1e-05

        def _gat_heads(x, adj, W, a):
            O = W.shape[-1]
            Wh = jnp.einsum('bnf,hfo->bhno', x, W)
            f1 = jnp.einsum('bhno,ho->bhn', Wh, a[:, :O])
            f2 = jnp.einsum('bhno,ho->bhn', Wh, a[:, O:])
            e = f1[:, :, :, None] + f2[:, :, None, :]
            e = jnp.where(e > 0, e, LEAKY_ALPHA * e)
            e = jnp.where(adj[None, None] > 0, e, NEG_INF)
            attn = jax.nn.softmax(e, axis=-1)
            return jnp.einsum('bhnm,bhmo->bhno', attn, Wh)
        B, N, _ = enc_inputs.shape
        h = jax.nn.elu(_gat_heads(enc_inputs, adj, W_heads, a_heads))
        h = jnp.transpose(h, (0, 2, 1, 3)).reshape(B, N, -1)
        out = _gat_heads(h, adj, W_out[None], a_out[None])[:, 0]
        out = jax.nn.elu(out)
        ffn = jnp.maximum(out @ w1 + b1, 0.0) @ w2 + b2
        y = ffn + out
        mu = jnp.mean(y, axis=-1, keepdims=True)
        var = jnp.var(y, axis=-1, keepdims=True)
        return (y - mu) / jnp.sqrt(var + LN_EPS) * ln_gamma + ln_beta

    def _L1_gnn_ref(x, adj, W, b):
        import jax, jax.numpy as jnp
        import numpy as np
        B, K, DIN, DOUT = (32, 64, 256, 256)
        Din = x.shape[-1]
        Wi, Wj = (W[:, :Din], W[:, Din:])
        mi = jnp.einsum('bkd,od->bko', x, Wi)
        mj = jnp.einsum('bkd,od->bko', x, Wj)
        a = adj.astype(x.dtype)
        deg = a.sum(axis=1)
        out = deg[None, :, None] * (mi + b) + jnp.einsum('ij,bjo->bio', a, mj)
        return out
    h = jnp.maximum(_layernorm(x, axis=-1), 0.0)
    x = x + _L0_gnn_ref(h, adj, L0_gnn_W_heads, L0_gnn_a_heads, L0_gnn_W_out, L0_gnn_a_out, L0_gnn_w1, L0_gnn_b1, L0_gnn_w2, L0_gnn_b2, L0_gnn_ln_gamma, L0_gnn_ln_beta)
    h = jnp.maximum(_layernorm(x, axis=-1), 0.0)
    x = x + _L1_gnn_ref(h, adj, L1_gnn_W, L1_gnn_b)
    return x

_drawn_inputs = setup_inputs


def setup_inputs(seed=0):
    import zlib

    import numpy as np

    out = dict(_drawn_inputs(seed))
    spreads = {'L0_gnn_b1': (0.0, 0.1),
     'L0_gnn_b2': (0.0, 0.1),
     'L0_gnn_ln_gamma': (1.0, 0.2),
     'L0_gnn_ln_beta': (0.0, 0.1)}
    factors = {}
    for name, (base, spread) in spreads.items():
        noise = np.random.default_rng([zlib.crc32(name.encode()), seed]).standard_normal(out[name].shape)
        drawn = base * np.exp(spread * noise) if base else spread * noise
        out[name] = jnp.asarray(drawn.astype(out[name].dtype))
    for name, factor in factors.items():
        out[name] = (out[name] * factor).astype(out[name].dtype)
    return out
```

```python
from contextlib import ExitStack

import concourse.bass as bass
from concourse import mybir



def gnn_kernel(nc, x, adj, W_heads, a_heads, W_out, a_out, w1, b1, w2, b2, gamma, beta, W_gc, b_gc, out):
    fp32, f32r, bf16, i32 = mybir.dt.float32, mybir.dt.float32r, mybir.dt.bfloat16, mybir.dt.int32
    ALU = mybir.AluOpType
    ACT = mybir.ActivationFunctionType
    AX = mybir.AxisListType

    P = 128
    B, N, F = x.shape
    H = W_heads.shape[0]
    NC = N // P
    KC = F // P
    OC = H * KC
    HN = N // 2
    FA = F + 2
    UN = 2 * H
    SLOPE = 0.01
    EPS = 1e-5
    BIG = 2.0 ** 100

    x_v = x.rearrange("b (c p) f -> b p c f", p=P)
    out_v = out.rearrange("b (c p) f -> b p c f", p=P)

    ctx = ExitStack()
    with ctx:
        def sb(name, shape, dt=fp32):
            return ctx.enter_context(nc.sbuf_tensor(name, shape, dt))

        def sem(name):
            return ctx.enter_context(nc.semaphore(name))

        wh = [sb(f"wh_{s}", [P, KC, H, FA], f32r) for s in ("hi", "lo")]
        wo = [sb(f"wo_{s}", [P, OC, FA], f32r) for s in ("hi", "lo")]
        w1_sb = sb("w1_sb", [P, KC, F])
        w2_sb = sb("w2_sb", [P, KC, F])
        wg = [sb(f"wg_{s}", [P, KC, 2 * F], f32r) for s in ("hi", "lo")]
        adjT = sb("adjT", [P, NC, N], f32r)
        maskT = sb("maskT", [P, NC, N], bf16)
        mask = sb("mask", [P, NC, N], bf16)
        deg = sb("deg", [P, NC])
        identb = sb("identb", [P, P], bf16)
        wsum = sb("wsum", [P, KC, H, 2])
        wsum2 = sb("wsum2", [P, OC, 2])
        cnt = sb("cnt", [P, NC])
        lone = sb("lone", [P, NC])
        degb = sb("degb", [P, NC, F])
        ident = sb("ident", [P, P])
        b1c = sb("b1c", [P, KC])
        b2_bc = sb("b2_bc", [P, F])
        gamma_bc = sb("gamma_bc", [P, F])
        beta_bc = sb("beta_bc", [P, F])
        pick = sb("pick", [P, 4, P], f32r)
        mhalf = sb("mhalf", [P, NC])

        xin = sb("xin", [P, NC, F])
        hT = [sb(f"hT_{s}", [P, KC, N], f32r) for s in ("hi", "lo")]
        whx = sb("whx_hi", [P, NC, H, FA], f32r)
        whl = sb("whx_lo", [P, NC, H, F], f32r)
        w2x = sb("w2x_hi", [P, NC, FA], f32r)
        w2l = sb("w2x_lo", [P, NC, F], f32r)
        arg = sb("arg", [P, 2, NC, HN])
        prob = [sb(f"prob_{s}", [P, 2, NC, HN], f32r) for s in ("hi", "lo")]
        elu_in = sb("elu_in", [P, 2, 2, F])
        elu_ex = sb("elu_ex", [P, 2, F])
        hcat = sb("hcat", [P, NC, H, F])
        hx = [sb(f"hx_{s}", [P, 8, P], f32r) for s in ("hi", "lo")]
        ff = sb("ff", [P, 2, NC, F])
        wk = sb("wk", [P, NC, F])
        xb = sb("xb", [P, NC, F])
        junk = sb("junk", [P, 4, N], bf16)
        held = sb("held", [P, 1])
        fcol = sb("fcol", [P, NC, H, 2])
        fcol2 = sb("fcol2", [P, NC, 1, 2])
        fs = sb("fs", [P, NC, H])
        fs2 = sb("fs2", [P, NC, 1])
        c1 = [sb(f"c1_{q}", [P, NC, 2, 2]) for q in range(3)]
        c2 = [sb(f"c2_{q}", [P, NC, 4, 2]) for q in range(3)]
        gmax = [sb(f"gmax_{q}", [P, NC, 2]) for q in range(3)]
        zrow = [sb(f"zrow_{q}", [P, 4, NC, 2]) for q in range(3)]
        f2row = sb("f2row", [P, N], f32r)
        rrow = [sb(f"rrow_{q}", [P, N], f32r) for q in range(3)]
        rec = sb("rec", [P, 2, 2])
        st = {k: sb(f"st_{k}", [P, NC, 6]) for k in ("in", "ff", "gc")}
        mv = {k: sb(f"mv_{k}", [P, NC, 2]) for k in ("in", "ff", "gc")}
        ve = {k: sb(f"ve_{k}", [P, NC]) for k in ("in", "ff", "gc")}
        rstd = {k: sb(f"rstd_{k}", [P, NC]) for k in ("in", "ff", "gc")}
        shift = {k: sb(f"shift_{k}", [P, NC]) for k in ("in", "ff", "gc")}

        pick_st = elu_in[:, :, :, :].rearrange("p a c f -> p (a c f)").rearrange("p (w h m) -> p w h m", w=2, h=2, m=2 * P)[:, :, :, 0:P]
        psA = [ctx.enter_context(nc.psum_tensor(f"psA{i}", [P, 2, 512], fp32)) for i in range(2)]
        psT = ctx.enter_context(nc.psum_tensor("psT", [P, 2, 512], fp32))
        psR = ctx.enter_context(nc.psum_tensor("psR", [P, 2, 512], fp32))

        NLOAD = 14
        ld = [sem(f"ld{i}") for i in range(NLOAD)]
        LD_ADJ, LD_WH, LD_A, LD_WO, LD_AO, LD_GC, LD_W1, LD_W2, LD_B1, LD_B2, LD_G, LD_BE, LD_BG, LD_A2 = range(NLOAD)
        s_zeroed = sem("s_zeroed")
        s_const = sem("s_const")
        s_picked = sem("s_picked")
        s_adj = sem("s_adj")
        s_adj_turned = sem("s_adj_turned")
        s_adj_out = sem("s_adj_out")
        s_gc_turned = sem("s_gc_turned")
        s_gc_hi = sem("s_gc_hi")
        s_setup = sem("s_setup")
        s_hi = sem("s_hi")
        s_dve = sem("s_dve")

        x_loaded = sem("x_loaded")
        ln_stat = {k: sem(f"ln_stat_{k}") for k in st}
        ln_aggr = {k: sem(f"ln_aggr_{k}") for k in st}
        ln_var = {k: sem(f"ln_var_{k}") for k in st}
        ln_rstd = {k: sem(f"ln_rstd_{k}") for k in st}
        ln_shift = {k: sem(f"ln_shift_{k}") for k in st}
        ln_out = {k: sem(f"ln_out_{k}") for k in st}
        h_turned = sem("h_turned")
        hT_hi = sem("hT_hi_ready")
        hT_lo = sem("hT_lo_ready")
        m1_done = sem("m1_done")
        m1_hi = sem("m1_hi")
        m1_lo = sem("m1_lo")
        m1_read = sem("m1_read")
        c1_made = [sem(f"c1_made{q}") for q in range(3)]
        c1_turned = [sem(f"c1_turned{q}") for q in range(3)]
        f2row_made = [sem(f"f2row_made{q}") for q in range(3)]
        f2_spread = [sem(f"f2_spread{q}") for q in range(3)]
        max_made = [sem(f"max_made{q}") for q in range(3)]
        row_math = [sem(f"row_math{q}") for q in range(3)]
        c2_turned = [sem(f"c2_turned{q}") for q in range(3)]
        rrow_made = [sem(f"rrow_made{q}") for q in range(3)]
        m2_turned = sem("m2_turned")
        hx_hi = sem("hx_hi_ready")
        hx_lo = sem("hx_lo_ready")
        m2_done = sem("m2_done")
        m2_hi = sem("m2_hi")
        m2_lo = sem("m2_lo")
        m2_read = sem("m2_read")
        xb_loaded = sem("xb_loaded")
        o_turned = sem("o_turned")
        oT_ready = sem("oT_ready")
        out_b2 = sem("out_b2")
        x_beta = sem("x_beta")
        f1_done = sem("f1_done")
        f1_read = sem("f1_read")
        f2_done = sem("f2_done")
        y_ready = sem("y_ready")
        y_gamma = sem("y_gamma")
        x2_ready = sem("x2_ready")
        x2_degb = sem("x2_degb")
        h2_turned = sem("h2_turned")
        h2_hi = sem("h2_hi")
        h2_lo = sem("h2_lo")
        conv_in = sem("conv_in")
        mj_hi = sem("mj_hi")
        mj_lo = sem("mj_lo")
        conv_in_read = sem("conv_in_read")
        conv_done = sem("conv_done")
        res_ready = sem("res_ready")
        stored = sem("stored")

        spread = sem("spread")
        arg_lin = sem("arg_lin")
        arg_max = sem("arg_max")
        arg_masked = sem("arg_masked")
        prob_hi = sem("prob_hi")
        prob_exp = sem("prob_exp")
        prob_lo = sem("prob_lo")
        att_done = sem("att_done")
        elu_rec = sem("elu_rec")
        elu_x = sem("elu_x")
        elu_neg = sem("elu_neg")
        elu_exp = sem("elu_exp")
        elu_out = sem("elu_out")

        block = ctx.enter_context(nc.Block())

        def wait(eng, s, count):
            if not isinstance(count, int) or count > 0:
                eng.wait_ge(s, count)

        BACK = -1

        def trip_order(front, heads, back):
            ahead = {
                4: [("norm_in", 1, 0)],
                5: [("norm_in_out", 1, 0), ("turn_in", 1, 0)],
                6: [("m1", 1, (0, 0)), ("m1", 1, (0, 1))],
                7: [("m1", 1, (1, 0)), ("m1", 1, (1, 1)), ("f2rows", 1, 0)],
                8: [("rowmax", 1, 0)],
                9: [("rows", 1, 0)],
            }
            own = {
                1: [("m1", 0, (2, 0)), ("m1", 0, (2, 1))],
                2: [("m1", 0, (3, 0)), ("m1", 0, (3, 1)), ("f2rows", 0, 1)],
                3: [("rowmax", 0, 1)],
                4: [("rows", 0, 1)],
            }
            behind = {
                0: [(name, -1, n) for n in range(NC) for name in ("turn2", "mix2")] + [("f2rows", -1, 2)],
                1: [("rowmax", -1, 2)],
                2: [("rows", -1, 2)],
                6: [("turn_out", -1, 0), ("ffn1", -1, 0)],
                7: [("ffn2", -1, 0), ("norm_ff", -1, 0)],
                8: [("norm_ff_out", -1, 0), ("norm_gc", -1, 0)],
                9: [("norm_gc_out", -1, 0), ("turn_gc", -1, 0), ("conv_in", -1, 0), ("conv_in", -1, 1), ("conv", -1, 0)],
            }
            seq = [(0, h, u) for h in range(2) for u in range(2)] + [(-1, BACK, 0), (-1, BACK, 1)] \
                + [(0, h, u) for h in range(2, 4) for u in range(2)]
            here = [(off, h, u) if (heads if off == 0 else back) else None for off, h, u in seq]
            steps = []

            def part(name, s):
                if 0 <= s < len(here) and here[s] is not None:
                    off, h, u = here[s]
                    if name == "args" and u == 0:
                        steps.append(("spread", off, (s, h, u)))
                    steps.append((name, off, (s, h, u)))

            if front:
                steps.append(("load", 1, 0))
            if back:
                steps.append(("load_back", -1, 0))
            part("args", 0)
            for s in range(len(seq)):
                part("args", s + 1)
                part("probs", s)
                part("elu_in", s - 1)
                part("elu_neg", s - 1)
                if heads:
                    steps.extend(own.get(s, []))
                if front:
                    steps.extend(ahead.get(s, []))
                part("elu_out", s - 1)
                if back:
                    steps.extend(behind.get(s, []))
                part("attend", s)
            part("elu_in", len(seq) - 1)
            part("elu_neg", len(seq) - 1)
            part("elu_out", len(seq) - 1)
            return steps

        class Place:
            pass

        def units_before(t):
            return 0 if isinstance(t, int) and t <= 0 else (UN + 2) * t - 2

        def run_trip(steps_of, t, front, heads, back, state):
            number, slot_of = {}, {}
            for name, off, info in trip_order(front, heads, back):
                c = Place()
                c.t, c.b, c.info, c.before = t, t + off, info, units_before(t)
                c.first = not heads and front
                key = (name, info)
                if name in ("spread", "args", "probs", "attend", "elu_in", "elu_neg", "elu_out"):
                    key, c.h, c.u = info
                    if name == "args":
                        number[key] = len(number)
                    c.nth = number.get(key, len(number))
                    c.unit, c.buf = c.before + c.nth, c.nth % 2
                elif name == "mix2":
                    key = (name, info // 2)
                if name in ("m1", "attend", "mix2", "ffn1", "ffn2", "conv_in") and key not in slot_of:
                    slot_of[key] = state["slot"]
                    state["slot"] ^= 1
                c.slot = slot_of.get(key)
                if name in steps_of:
                    steps_of[name](c)

        def run_all(eng, steps_of, at_trip_end=lambda: None):
            state = {"slot": 0}

            def trip(t, front, heads, back):
                run_trip(steps_of, t, front, heads, back, state)
                at_trip_end()

            trip(-1, True, False, False)
            trip(0, True, True, False)
            trip(1, True, True, True)
            slot = state["slot"]
            with eng.Fori(2, B - 1) as t:
                trip(t, True, True, True)
            assert state["slot"] == slot
            trip(B - 1, False, True, True)
            trip(B, False, False, True)

        def heads_of(q):
            return (0, 2) if q == 0 else (2, 2) if q == 1 else (0, 1)

        @block.sync
        def _(sp):
            sp.dma_start(arg[:, :, :, :].rearrange("p a c n -> p (a c n)").bitcast(i32).rearrange("p (c n) -> p c n", c=NC),
                         adj.rearrange("(c p) n -> p c n", p=P)).then_inc(ld[LD_ADJ], 16)
            sp.dma_start(xb[:, :, :].rearrange("p (a c) f -> p a (c f)", a=2), W_gc.rearrange("(a p) d -> p a d", p=P)).then_inc(ld[LD_GC], 16)
            for k in range(KC):
                sp.dma_start(hcat[:, k, :, :], W_heads[:, k * P:(k + 1) * P, :].rearrange("h p o -> p h o")).then_inc(ld[LD_WH], 16)
            sp.dma_start(ff[:, :, :, :].rearrange("p a c f -> p (a c f)").rearrange("p (h f) -> p h f", h=H),
                         a_heads.partition_broadcast(P)).then_inc(ld[LD_A], 16)
            sp.dma_start(hcat[:, KC:NC, :, :].rearrange("p a h f -> p (a h) f"), W_out.rearrange("(k p) o -> p k o", p=P)).then_inc(ld[LD_WO], 16)
            sp.dma_start(wk[:, 0:2, :].rearrange("p c f -> p (c f)"), a_out.partition_broadcast(P)).then_inc(ld[LD_AO], 16)
            sp.dma_start(wk[:, 2, :], b_gc.partition_broadcast(P)).then_inc(ld[LD_BG], 16)
            sp.dma_start(w1_sb[:, :, :], w1.rearrange("(k p) o -> p k o", p=P)).then_inc(ld[LD_W1], 16)
            sp.dma_start(w2_sb[:, :, :], w2.rearrange("(k p) o -> p k o", p=P)).then_inc(ld[LD_W2], 16)
            sp.dma_start(b1c[:, :], b1.rearrange("(k p) -> p k", p=P), allow_slow_non_contiguous=True).then_inc(ld[LD_B1], 16)
            sp.dma_start(b2_bc[:, :], b2.partition_broadcast(P)).then_inc(ld[LD_B2], 16)
            sp.dma_start(gamma_bc[:, :], gamma.partition_broadcast(P)).then_inc(ld[LD_G], 16)
            sp.dma_start(beta_bc[:, :], beta.partition_broadcast(P)).then_inc(ld[LD_BE], 16)

            def load(c):
                wait(sp, h_turned, c.b)
                sp.dma_start(xin[:, :, :], x_v[c.b]).then_inc(x_loaded, 16)

            def load_back(c):
                wait(sp, s_setup, 1)
                wait(sp, stored, 16 * c.b)
                sp.dma_start(xb[:, :, :], x_v[c.b]).then_inc(xb_loaded, 16)

            def conv(c):
                wait(sp, res_ready, c.b + 1)
                sp.dma_start(out_v[c.b], xb[:, :, :]).then_inc(stored, 16)

            run_all(sp, {"load": load, "load_back": load_back, "conv": conv})
            sp.wait_ge(stored, 16 * B)

        @block.gpsimd
        def _(pool):
            pool.memset(ident[:, :], 0.0).then_inc(s_zeroed, 1)
            pool.memset(mhalf[:, :], -0.5).then_inc(s_zeroed, 1)
            pool.memset(pick_st, 0.0).then_inc(s_zeroed, 1)
            pool.wait_ge(s_zeroed, 3)
            pool.affine_select(out=ident[:, :], in_=ident[:, :], compare_op=ALU.not_equal, fill=1.0, base=0,
                               pattern=[[-1, P]], channel_multiplier=1).then_inc(s_const, 1)
            for z in range(2):
                pool.affine_select(out=pick_st, in_=pick_st, compare_op=ALU.not_equal, fill=1.0, base=-2 * z,
                                   pattern=[[-4, 2], [-1, 2], [0, P]], channel_multiplier=1).then_inc(s_const, 1)
                pool.wait_ge(s_const, 2 + z)

            def norm(k):
                def step(c):
                    pool.wait_ge(ln_var[k], c.b + 1)
                    pool.tensor_tensor(out=rstd[k][:, :], in0=ve[k][:, :], in1=mhalf[:, :], op=ALU.pow).then_inc(ln_rstd[k], 1)
                return step

            def args(c):
                pool.wait_ge(arg_max, NC * (c.unit + 1))
                a = arg[:, c.buf, :, :]
                pool.tensor_tensor(out=a, in0=a, in1=maskT[:, :, c.u * HN:(c.u + 1) * HN], op=ALU.add).then_inc(arg_masked, 1)

            def turn_out(c):
                pool.wait_ge(xb_loaded, 16 * (c.b + 1))
                pool.tensor_tensor(out=xb[:, :, :], in0=xb[:, :, :], in1=beta_bc[:, None, :].to_broadcast([P, NC, F]),
                                   op=ALU.add).then_inc(x_beta, 1)
                pool.wait_ge(o_turned, c.b + 1)
                pool.tensor_tensor(out=wk[:, :, :], in0=wk[:, :, :], in1=b2_bc[:, None, :].to_broadcast([P, NC, F]),
                                   op=ALU.add).then_inc(out_b2, 1)

            def norm_ff_out(c):
                pool.wait_ge(ln_out["ff"], c.b + 1)
                pool.tensor_tensor(out=wk[:, :, :], in0=wk[:, :, :], in1=gamma_bc[:, None, :].to_broadcast([P, NC, F]),
                                   op=ALU.mult).then_inc(y_gamma, 1)

            def norm_gc_out(c):
                pool.wait_ge(ln_out["gc"], c.b + 1)
                pool.tensor_tensor(out=xb[:, :, :], in0=xb[:, :, :], in1=degb[:, :, :], op=ALU.add).then_inc(x2_degb, 1)

            for l in (LD_B2, LD_G, LD_BE):
                pool.wait_ge(ld[l], 16)
            pool.wait_ge(s_setup, 1)
            run_all(pool, {"norm_in": norm("in"), "args": args, "turn_out": turn_out, "norm_ff": norm("ff"),
                           "norm_ff_out": norm_ff_out, "norm_gc": norm("gc"),
                           "norm_gc_out": norm_gc_out})

        @block.scalar
        def _(act):
            act.wait_ge(ld[LD_WH], 16 * KC)
            act.activation(wh[0][:, :, :, 0:F], hcat[:, 0:KC, :, :], ACT.Copy).then_inc(s_hi, 1)
            act.wait_ge(ld[LD_WO], 16)
            act.activation(wo[0][:, :, 0:F], hcat[:, KC:NC, :, :].rearrange("p a h f -> p (a h) f"), ACT.Copy).then_inc(s_hi, 1)
            act.wait_ge(s_gc_turned, 1)
            act.activation(wg[0][:, :, :], psR[:, :, :], ACT.Copy).then_inc(s_gc_hi, 1)
            act.wait_ge(ld[LD_B1], 16)
            act.wait_ge(s_setup, 1)

            def norm_out(k, src, dst, func):
                def step(c):
                    act.wait_ge(ln_shift[k], c.b + 1)
                    for n in range(NC):
                        i = act.activation(dst[:, n, :], src[:, n, :], func, bias=shift[k][:, n:n + 1],
                                           scale=rstd[k][:, n:n + 1])
                    i.then_inc(ln_out[k], 1)
                return step

            def turn_in(c):
                act.wait_ge(h_turned, c.b + 1)
                wait(act, m1_done, 2 * H * c.b)
                act.activation(hT[0][:, :, :], psT[:, :, :], ACT.Copy).then_inc(hT_hi, 1)

            def m1(c):
                h, p = c.info
                act.wait_ge(m1_done, 2 * H * c.b + 2 * h + p + 1)
                wait(act, att_done, c.before + (2 * h + 2 if h < 2 and not c.first else 0))
                act.activation(whx[:, 2 * p:2 * p + 2, h, 0:F], psA[c.slot][:, :, 0:F], ACT.Copy).then_inc(m1_hi, 1)

            def f2rows(c):
                q = c.info
                act.wait_ge(c1_turned[q], c.b + 1)
                act.activation(f2row[0:4, :], psT[0:4, 0, :], ACT.Copy).then_inc(f2row_made[q], 1)

            def rows(c):
                q = c.info
                act.wait_ge(c2_turned[q], c.b + 1)
                wait(act, spread, c.before + (4 if q == 0 and not c.first else 0))
                act.activation(rrow[q][0:8, :], psT[0:8, 0, :], ACT.Copy).then_inc(rrow_made[q], 1)

            def args(c):
                act.wait_ge(spread, c.unit - c.u + 2)
                wait(act, prob_lo, c.unit - 1)
                f = fs2[:, :, 0] if c.h == BACK else fs[:, :, c.h]
                for j in range(NC):
                    act.activation(arg[:, c.buf, j, :], psR[:, 1, c.u * HN:(c.u + 1) * HN], ACT.Identity,
                                   bias=f[:, j:j + 1]).then_inc(arg_lin, 1)

            def probs(c):
                act.wait_ge(arg_masked, c.unit + 1)
                wait(act, att_done, c.unit - 1)
                act.activation(prob[0][:, c.buf, :, :], arg[:, c.buf, :, :], ACT.Exp).then_inc(prob_hi, 1)
                act.activation(arg[:, c.buf, :, :], arg[:, c.buf, :, :], ACT.Exp).then_inc(prob_exp, 1)

            def elu_in_(c):
                act.wait_ge(elu_rec, c.unit + 1)
                wait(act, elu_out, c.unit - 1)
                for n in range(2):
                    i = act.activation(elu_in[:, c.buf, n, :], psA[c.slot][:, n, 0:F], ACT.Copy,
                                       scale=rec[:, c.buf, n:n + 1])
                i.then_inc(elu_x, 1)

            def elu_out_(c):
                act.wait_ge(elu_neg, c.unit + 1)
                act.activation(elu_ex[:, :, :], elu_ex[:, :, :], ACT.Exp).then_inc(elu_exp, 1)

            def turn2(c):
                act.wait_ge(m2_turned, NC * c.b + c.info + 1)
                wait(act, m2_done, NC * c.b + c.info)
                if c.info == 0:
                    wait(act, conv_in, 2 * c.b)
                act.activation(hx[0][:, :, :], psT[:, :, :].rearrange("p a n -> p (a n)").rearrange("p (k n) -> p k n", k=OC),
                               ACT.Copy).then_inc(hx_hi, 1)

            def mix2(c):
                if c.info % 2:
                    act.wait_ge(m2_done, NC * c.b + c.info + 1)
                    wait(act, conv_done, c.b)
                    act.activation(w2x[:, c.info - 1:c.info + 1, 0:F], psA[c.slot][:, :, 0:F], ACT.Copy).then_inc(m2_hi, 1)

            def turn_out(c):
                act.wait_ge(o_turned, c.b + 1)
                act.activation(ff[:, 0, :, :], psT[:, :, :].rearrange("p a n -> p (a n)").rearrange("p (k n) -> p k n", k=NC),
                               ACT.Copy).then_inc(oT_ready, 1)

            def ffn1(c):
                for o in range(KC):
                    act.wait_ge(f1_done, KC * c.b + o + 1)
                    act.activation(ff[:, 1, 2 * o:2 * o + 2, :].rearrange("p c f -> p (c f)"), psA[c.slot][:, o, :], ACT.Relu,
                                   bias=b1c[:, o:o + 1]).then_inc(f1_read, 1)

            def turn_gc(c):
                act.wait_ge(h2_turned, c.b + 1)
                act.wait_ge(m2_done, NC * (c.b + 1))
                act.activation(hx[0][:, :, :], psT[:, :, :].rearrange("p a n -> p (a n)").rearrange("p (k n) -> p k n", k=OC),
                               ACT.Copy).then_inc(h2_hi, 1)

            def conv_in_(c):
                act.wait_ge(conv_in, 2 * c.b + c.info + 1)
                act.activation(w2x[:, 2 * c.info:2 * c.info + 2, 0:F], psA[c.slot][:, :, F:2 * F], ACT.Copy).then_inc(mj_hi, 1)

            run_all(act, {"norm_in_out": norm_out("in", xin, xin, ACT.Relu), "turn_in": turn_in, "m1": m1, "f2rows": f2rows,
                          "rows": rows, "args": args, "probs": probs, "elu_in": elu_in_, "elu_out": elu_out_,
                          "turn2": turn2, "mix2": mix2, "turn_out": turn_out, "ffn1": ffn1,
                          "norm_ff_out": norm_out("ff", wk, wk, ACT.Identity),
                          "norm_gc_out": norm_out("gc", xb, ff[:, 1, :, :], ACT.Relu),
                          "turn_gc": turn_gc, "conv_in": conv_in_})

        @block.vector
        def _(dve):
            count = [0]

            def link(ins):
                count[0] += 1
                ins.then_inc(s_dve, 1)
                dve.wait_ge(s_dve, count[0])

            adj_f = arg[:, :, :, :].rearrange("p a c n -> p (a c n)").rearrange("p (c n) -> p c n", c=NC)
            dve.wait_ge(ld[LD_ADJ], 16)
            link(dve.tensor_copy(adj_f, adj_f.bitcast(i32)))
            dve.tensor_scalar(mask[:, :, :], adj_f, 0.0, 1.0, ALU.is_gt, ALU.mult).then_inc(s_adj, 1)
            link(dve.tensor_reduce(out=deg[:, :], in_=adj_f, axis=AX.X, op=ALU.add))
            dve.wait_ge(s_adj, 1)
            link(dve.tensor_reduce(out=cnt[:, :], in_=mask[:, :, :], axis=AX.X, op=ALU.add))
            link(dve.tensor_scalar(lone[:, :], cnt[:, :], 0.0, 2.0 * BIG, ALU.is_equal, ALU.mult))
            link(dve.tensor_scalar(lone[:, :], lone[:, :], -BIG, None, ALU.add))
            dve.wait_ge(s_const, 3)
            link(dve.tensor_copy(identb[:, :], ident[:, :]))
            for n in range(NC):
                dve.tensor_scalar(mask[:, n, :], mask[:, n, :], BIG, lone[:, n:n + 1], ALU.mult, ALU.add).then_inc(s_adj, 1)
            link(dve.tensor_copy(pick[:, :, :].rearrange("p (w h) m -> p w h m", w=2), pick_st))
            dve.memset(f2row[:, :].bitcast(fp32), 0.0)
            for q in range(3):
                dve.memset(rrow[q][:, :].bitcast(fp32), 0.0)
                dve.memset(c1[q][:, :, :, :], 0.0)
                dve.memset(c2[q][:, :, :, :], 0.0)
            dve.memset(whx[:, :, :, F:FA].bitcast(fp32), 1.0)
            link(dve.memset(w2x[:, :, F:FA].bitcast(fp32), 1.0))
            for n in range(NC):
                dve.wait_ge(s_adj_turned, n + 1)
                dve.tensor_copy(adjT[:, :, n * P:(n + 1) * P], psT[:, n % 2, :].rearrange("p (j i) -> p j i", j=NC))
                dve.tensor_copy(maskT[:, :, n * P:(n + 1) * P],
                                psA[n % 2][:, 0, 0:N // 2].bitcast(bf16).rearrange("p (j i) -> p j i", j=NC)).then_inc(s_adj_out, 1)
            dve.wait_ge(s_gc_hi, 1)
            dve.tensor_tensor(out=wg[1][:, :, :], in0=psR[:, :, :], in1=wg[0][:, :, :].bitcast(fp32), op=ALU.subtract)
            dve.wait_ge(ld[LD_BG], 16)
            for n in range(NC):
                dve.tensor_scalar(degb[:, n, :], wk[:, 2, :], deg[:, n:n + 1], None, ALU.mult)
            a_h = ff[:, :, :, :].rearrange("p a c f -> p (a c f)").rearrange("p (h s f) -> p h s f", h=H, s=2)
            a_o = wk[:, 0:2, :]
            w_o = hcat[:, KC:NC, :, :].rearrange("p a h f -> p (a h) f")
            dve.wait_ge(ld[LD_WH], 16 * KC)
            for l in (LD_A, LD_WO, LD_AO):
                dve.wait_ge(ld[l], 16)
            for s in range(2):
                for k in range(KC):
                    for h in range(H):
                        link(dve.tensor_tensor_reduce(out=junk[:, 0, 0:F], in0=hcat[:, k, h, :], in1=a_h[:, h, s, :], scale=1.0,
                                                      scalar=0.0, op0=ALU.mult, op1=ALU.add, accum_out=wsum[:, k, h, s:s + 1]))
                for k in range(OC):
                    link(dve.tensor_tensor_reduce(out=junk[:, 0, 0:F], in0=w_o[:, k, :], in1=a_o[:, s, :], scale=1.0,
                                                  scalar=0.0, op0=ALU.mult, op1=ALU.add, accum_out=wsum2[:, k, s:s + 1]))
            dve.tensor_copy(wh[0][:, :, :, F:FA], wsum[:, :, :, :])
            link(dve.tensor_copy(wo[0][:, :, F:FA], wsum2[:, :, :]))
            dve.wait_ge(s_hi, 2)
            for k in range(KC):
                dve.tensor_tensor(out=wh[1][:, k, :, F:FA], in0=wsum[:, k, :, :], in1=wh[0][:, k, :, F:FA].bitcast(fp32), op=ALU.subtract)
                dve.tensor_tensor(out=wh[1][:, k, :, 0:F], in0=hcat[:, k, :, :], in1=wh[0][:, k, :, 0:F].bitcast(fp32), op=ALU.subtract)
            dve.tensor_tensor(out=wo[1][:, :, F:FA], in0=wsum2[:, :, :], in1=wo[0][:, :, F:FA].bitcast(fp32), op=ALU.subtract)
            link(dve.tensor_tensor(out=wo[1][:, :, 0:F], in0=w_o, in1=wo[0][:, :, 0:F].bitcast(fp32), op=ALU.subtract))
            dve.memset(junk[:, 0, 0:2], 0.0).then_inc(s_setup, 1)

            def norm(k, src, ready, per):
                def step(c):
                    dve.wait_ge(ready, per * (c.b + 1))
                    for n in range(NC):
                        i = dve.bn_stats(st[k][:, n, :], src[:, n, :])
                    i.then_inc(ln_stat[k], 1)
                    dve.wait_ge(s_setup, 1)
                    dve.wait_ge(ln_stat[k], c.b + 1)
                    for n in range(NC):
                        i = dve.bn_aggr(mv[k][:, n, :], st[k][:, n, :])
                    i.then_inc(ln_aggr[k], 1)
                    dve.wait_ge(ln_aggr[k], c.b + 1)
                    dve.tensor_scalar(ve[k][:, :], mv[k][:, :, 1], EPS, None, ALU.add).then_inc(ln_var[k], 1)
                return step

            def norm_out(k):
                def step(c):
                    dve.wait_ge(ln_rstd[k], c.b + 1)
                    dve.scalar_tensor_tensor(out=shift[k][:, :], in0=mv[k][:, :, 0], scalar=-1.0, in1=rstd[k][:, :],
                                             op0=ALU.mult, op1=ALU.mult).then_inc(ln_shift[k], 1)
                return step

            def lo(dst, src, hi):
                return dve.tensor_tensor(out=dst, in0=src, in1=hi.bitcast(fp32), op=ALU.subtract)

            def turn_in(c):
                dve.wait_ge(hT_hi, c.b + 1)
                lo(hT[1][:, :, :], psT[:, :, :], hT[0][:, :, :]).then_inc(hT_lo, 1)

            def m1(c):
                h, p = c.info
                dve.wait_ge(m1_hi, 2 * H * c.b + 2 * h + p + 1)
                ps = psA[c.slot]
                lo(whl[:, 2 * p:2 * p + 2, h, :], ps[:, :, 0:F], whx[:, 2 * p:2 * p + 2, h, 0:F]).then_inc(m1_lo, 1)
                dve.tensor_copy(fcol[:, 2 * p:2 * p + 2, h, :], ps[:, :, F:FA]).then_inc(m1_read, 1)

            def cols(q):
                h0, nh = heads_of(q)
                return (fcol2 if q == 2 else fcol)[:, :, h0:h0 + nh, :], (fs2 if q == 2 else fs)[:, :, h0:h0 + nh], nh

            def f2rows(c):
                q = c.info
                f, f_s, nh = cols(q)
                if q == 2:
                    dve.wait_ge(m2_read, 2 * (c.b + 1))
                else:
                    dve.wait_ge(m1_read, 2 * H * c.b + 4 * q + 4)
                dve.tensor_scalar(f_s, f[:, :, :, 1], SLOPE, None, ALU.mult).then_inc(c1_made[q], 1)
                dve.tensor_copy(c1[q][:, :, 0, 0:nh].bitcast(f32r), f[:, :, :, 1]).then_inc(c1_made[q], 1)
                dve.wait_ge(c1_made[q], 3 * c.b + 2)
                dve.tensor_tensor(out=c1[q][:, :, 1, 0:nh], in0=f[:, :, :, 1], in1=c1[q][:, :, 0, 0:nh],
                                  op=ALU.subtract).then_inc(c1_made[q], 1)

            def rowmax(c):
                q = c.info
                f, _, nh = cols(q)
                dve.wait_ge(f2_spread[q], c.b + 1)
                dve.memset(held[:, :], 0.0)
                for k in range(nh * NC):
                    hh, n = k // NC, k % NC
                    if k == 4:
                        dve.wait_ge(max_made[q], nh * NC * c.b + k)
                        dve.memset(held[:, :], 0.0)
                    dve.tensor_tensor_reduce(out=junk[:, k % 4, :], in0=psT[:, hh, :], in1=mask[:, n, :], scale=1.0,
                                             scalar=-3.0e38, op0=ALU.add, op1=ALU.max,
                                             accum_out=gmax[q][:, n, hh:hh + 1]).then_inc(max_made[q], 1)
                dve.wait_ge(max_made[q], nh * NC * (c.b + 1))
                z, m, ra, rb = (zrow[q][:, k, :, 0:nh] for k in range(4))
                f1 = f[:, :, :, 0]
                g = gmax[q][:, :, 0:nh]
                done = row_math[q]

                def after(k):
                    dve.wait_ge(done, 8 * c.b + k)

                dve.tensor_tensor(out=z, in0=f1, in1=g, op=ALU.add).then_inc(done, 1)
                after(1)
                dve.scalar_tensor_tensor(out=m, in0=z, scalar=SLOPE, in1=z, op0=ALU.mult, op1=ALU.max).then_inc(done, 1)
                after(2)
                dve.tensor_tensor(out=ra, in0=f1, in1=m, op=ALU.subtract).then_inc(done, 1)
                dve.scalar_tensor_tensor(out=rb, in0=f1, scalar=SLOPE, in1=m, op0=ALU.mult, op1=ALU.subtract).then_inc(done, 1)
                k = [c2[q][:, :, i, 0:nh] for i in range(4)]
                after(3)
                dve.tensor_copy(k[0].bitcast(f32r), ra).then_inc(done, 1)
                after(4)
                dve.tensor_copy(k[2].bitcast(f32r), rb).then_inc(done, 1)
                after(5)
                dve.tensor_tensor(out=k[1], in0=ra, in1=k[0], op=ALU.subtract).then_inc(done, 1)
                after(6)
                dve.tensor_tensor(out=k[3], in0=rb, in1=k[2], op=ALU.subtract).then_inc(done, 1)

            def args(c):
                f = fcol2[:, :, 0, 1] if c.h == BACK else fcol[:, :, c.h, 1]
                for j in range(NC):
                    dve.wait_ge(arg_lin, NC * c.unit + j + 1)
                    a = arg[:, c.buf, j, :]
                    dve.scalar_tensor_tensor(out=a, in0=psR[:, 0, c.u * HN:(c.u + 1) * HN], scalar=f[:, j:j + 1], in1=a,
                                             op0=ALU.add, op1=ALU.max).then_inc(arg_max, 1)

            def probs(c):
                dve.wait_ge(prob_exp, c.unit + 1)
                lo(prob[1][:, c.buf, :, :], arg[:, c.buf, :, :], prob[0][:, c.buf, :, :]).then_inc(prob_lo, 1)

            def elu_in_(c):
                dve.wait_ge(att_done, c.unit + 1)
                dve.reciprocal(rec[:, c.buf, :], psA[c.slot][:, :, F]).then_inc(elu_rec, 1)

            def elu_neg_(c):
                dve.wait_ge(elu_x, c.unit + 1)
                wait(dve, elu_out, c.unit)
                dve.tensor_scalar(elu_ex[:, :, :], elu_in[:, c.buf, :, :], 0.0, None, ALU.min).then_inc(elu_neg, 1)

            def elu_out_(c):
                dve.wait_ge(elu_exp, c.unit + 1)
                if c.h == BACK:
                    dst = wk[:, 2 * c.u:2 * c.u + 2, :]
                else:
                    wait(dve, m2_turned, NC * c.b)
                    dst = hcat[:, 2 * c.u:2 * c.u + 2, c.h, :]
                dve.scalar_tensor_tensor(out=dst, in0=elu_ex[:, :, :], scalar=-1.0, in1=elu_in[:, c.buf, :, :],
                                         op0=ALU.add, op1=ALU.max).then_inc(elu_out, 1)

            hx_of_T = psT[:, :, :].rearrange("p a n -> p (a n)").rearrange("p (k n) -> p k n", k=OC)

            def turn2(c):
                dve.wait_ge(hx_hi, NC * c.b + c.info + 1)
                lo(hx[1][:, :, :], hx_of_T, hx[0][:, :, :]).then_inc(hx_lo, 1)

            def mix2(c):
                if c.info % 2:
                    dve.wait_ge(m2_hi, 2 * c.b + c.info // 2 + 1)
                    ps, n = psA[c.slot], c.info - 1
                    lo(w2l[:, n:n + 2, :], ps[:, :, 0:F], w2x[:, n:n + 2, 0:F]).then_inc(m2_lo, 1)
                    dve.tensor_copy(fcol2[:, n:n + 2, 0, :], ps[:, :, F:FA]).then_inc(m2_read, 1)

            def ffn2(c):
                dve.wait_ge(f2_done, c.b + 1)
                dve.wait_ge(out_b2, c.b + 1)
                dve.tensor_tensor(out=wk[:, :, :], in0=psA[c.slot][:, :, :].rearrange("p a (c f) -> p (a c) f", c=2), in1=wk[:, :, :],
                                  op=ALU.add).then_inc(y_ready, 1)

            def norm_ff_out(c):
                norm_out("ff")(c)
                dve.wait_ge(y_gamma, c.b + 1)
                dve.wait_ge(x_beta, c.b + 1)
                dve.tensor_tensor(out=xb[:, :, :], in0=xb[:, :, :], in1=wk[:, :, :], op=ALU.add).then_inc(x2_ready, 1)

            def turn_gc(c):
                dve.wait_ge(h2_hi, c.b + 1)
                lo(hx[1][:, :, :], hx_of_T, hx[0][:, :, :]).then_inc(h2_lo, 1)

            def conv_in_(c):
                p, ps = c.info, psA[c.slot]
                dve.wait_ge(mj_hi, 2 * c.b + p + 1)
                lo(w2l[:, 2 * p:2 * p + 2, :], ps[:, :, F:2 * F], w2x[:, 2 * p:2 * p + 2, 0:F]).then_inc(mj_lo, 1)
                dve.wait_ge(x2_degb, c.b + 1)
                for i in range(2):
                    n = 2 * p + i
                    r = dve.scalar_tensor_tensor(out=xb[:, n, :], in0=ps[:, i, 0:F], scalar=deg[:, n:n + 1], in1=xb[:, n, :],
                                                 op0=ALU.mult, op1=ALU.add)
                r.then_inc(conv_in_read, 1)

            def conv(c):
                dve.wait_ge(conv_done, c.b + 1)
                dve.wait_ge(conv_in_read, 2 * (c.b + 1))
                dve.tensor_tensor(out=xb[:, :, :], in0=psT[:, :, :].rearrange("p a (c f) -> p (a c) f", c=2), in1=xb[:, :, :],
                                  op=ALU.add).then_inc(res_ready, 1)

            run_all(dve, {"norm_in": norm("in", xin, x_loaded, 16), "norm_in_out": norm_out("in"), "turn_in": turn_in, "m1": m1,
                          "f2rows": f2rows, "rowmax": rowmax, "args": args, "probs": probs, "elu_in": elu_in_, "elu_neg": elu_neg_,
                          "elu_out": elu_out_, "turn2": turn2, "mix2": mix2, "ffn2": ffn2, "norm_ff": norm("ff", wk, y_ready, 1),
                          "norm_ff_out": norm_ff_out, "norm_gc": norm("gc", xb, x2_ready, 1), "norm_gc_out": norm_out("gc"),
                          "turn_gc": turn_gc, "conv_in": conv_in_, "conv": conv})

        @block.tensor
        def _(pe):
            adj_f = arg[:, :, :, :].rearrange("p a c n -> p (a c n)").rearrange("p (c n) -> p c n", c=NC)
            pe.wait_ge(s_const, 3)
            pe.wait_ge(s_adj, 1 + NC)
            for n in range(NC):
                wait(pe, s_adj_out, n - 1)
                for j in range(NC):
                    pe.transpose(psT[:, n % 2, j * P:(j + 1) * P], adj_f[:, n, j * P:(j + 1) * P], ident[:, :])
                    i = pe.transpose(psA[n % 2][:, 0, j * P // 2:(j + 1) * P // 2].bitcast(bf16), mask[:, n, j * P:(j + 1) * P], identb[:, :])
                i.then_inc(s_adj_turned, 1)
            pe.wait_ge(ld[LD_GC], 16)
            w_gc = xb[:, :, :].rearrange("p (a c) f -> p a (c f)", a=2)
            for k in range(KC):
                for side in range(2):
                    for o in range(KC):
                        i = pe.transpose(psR[:, k, side * F + o * P:side * F + (o + 1) * P],
                                         w_gc[:, o, side * F + k * P:side * F + (k + 1) * P], ident[:, :])
            i.then_inc(s_gc_turned, 1)
            for l in (LD_W1, LD_W2):
                pe.wait_ge(ld[l], 16)
            pe.wait_ge(s_setup, 1)

            lent = {}

            def take(ps, t):
                if ps in lent:
                    s, at, ago = lent[ps]
                    wait(pe, s, at(t - ago))

            def lend(ps, s, at):
                lent[ps] = (s, at, 0)

            def at_trip_end():
                for ps, (s, at, ago) in lent.items():
                    lent[ps] = (s, at, ago + 1)

            def product(out, steps, wide=None):
                n = 3 * len(steps)
                k = 0
                for lh, ll, rh, rl in steps:
                    for a, b_, o in ((lh, rh, wide if wide is not None else out), (ll, rh, wide if wide is not None else out), (lh, rl, out)):
                        i = pe.matmul(o, a, b_, start=(k == 0), stop=(k == n - 1))
                        k += 1
                return i

            def turn_in(c):
                pe.wait_ge(ln_out["in"], c.b + 1)
                take("T", c.t)
                for k in range(KC):
                    for n in range(NC):
                        i = pe.transpose(psT[:, k, n * P:(n + 1) * P], xin[:, n, k * P:(k + 1) * P], ident[:, :])
                i.then_inc(h_turned, 1)
                lend("T", hT_lo, lambda t: t + 2)

            def m1(c):
                h, p = c.info
                pe.wait_ge(hT_lo, c.b + 1)
                take(c.slot, c.t)
                for i in range(2):
                    n = 2 * p + i
                    r = product(psA[c.slot][:, i, 0:FA],
                                [(hT[0][:, k, n * P:(n + 1) * P], hT[1][:, k, n * P:(n + 1) * P], wh[0][:, k, h, :], wh[1][:, k, h, :])
                                 for k in range(KC)])
                r.then_inc(m1_done, 1)
                off = 1 if h < 2 else 0
                lend(c.slot, m1_read, lambda t: 2 * H * (t + off) + 2 * h + p + 1)

            def f2rows(c):
                q = c.info
                pe.wait_ge(c1_made[q], 3 * (c.b + 1))
                take("T", c.t)
                for n in range(NC):
                    i = pe.transpose(psT[0:4, 0, n * P:(n + 1) * P], c1[q][:, n, :, :].rearrange("p a h -> p (a h)"), ident[:, :])
                i.then_inc(c1_turned[q], 1)
                off = (1, 0, -1)[q]
                lend("T", f2row_made[q], lambda t: t + off + 1)

            def rowmax(c):
                q = c.info
                nh = heads_of(q)[1]
                pe.wait_ge(f2row_made[q], c.b + 1)
                take("T", c.t)
                for hh in range(nh):
                    i = pe.matmul(psT[:, hh, :], pick[:, hh, :], f2row[:, :], start=True, stop=True)
                i.then_inc(f2_spread[q], 1)
                off = (1, 0, -1)[q]
                lend("T", max_made[q], lambda t: nh * NC * (t + off + 1))

            def rows(c):
                q = c.info
                pe.wait_ge(row_math[q], 8 * (c.b + 1))
                take("T", c.t)
                for n in range(NC):
                    i = pe.transpose(psT[0:8, 0, n * P:(n + 1) * P], c2[q][:, n, :, :].rearrange("p a h -> p (a h)"), ident[:, :])
                i.then_inc(c2_turned[q], 1)
                off = (1, 0, -1)[q]
                lend("T", rrow_made[q], lambda t: t + off + 1)

            def spread_(c):
                q, hh = (2, 0) if c.h == BACK else (c.h // 2, c.h % 2)
                pe.wait_ge(rrow_made[q], c.b + 1)
                wait(pe, arg_max, NC * c.unit)
                for w in range(2):
                    pe.matmul(psR[:, w, :], pick[:, 2 * w + hh, :], rrow[q][:, :], start=True, stop=True).then_inc(spread, 1)

            def attend(c):
                pe.wait_ge(prob_lo, c.unit + 1)
                if c.h == BACK:
                    pe.wait_ge(m2_read, 2 * (c.b + 1))
                    hi, low = (lambda j: w2x[:, j, :]), (lambda j: w2l[:, j, :])
                else:
                    pe.wait_ge(m1_read, 2 * H * c.b + 2 * c.h + 2)
                    hi, low = (lambda j: whx[:, j, c.h, :]), (lambda j: whl[:, j, c.h, :])
                take(c.slot, c.t)
                for n in range(2):
                    r = product(psA[c.slot][:, n, 0:F],
                                [(prob[0][:, c.buf, j, n * P:(n + 1) * P], prob[1][:, c.buf, j, n * P:(n + 1) * P], hi(j), low(j))
                                 for j in range(NC)], wide=psA[c.slot][:, n, 0:FA])
                r.then_inc(att_done, 1)
                nth = c.nth
                lend(c.slot, elu_x, lambda t: units_before(t) + nth + 1)

            def turn2(c):
                pe.wait_ge(elu_out, c.before)
                take("T", c.t)
                for k in range(OC):
                    i = pe.transpose(psT[:, k // 4, (k % 4) * P:(k % 4 + 1) * P], hcat[:, c.info, k // KC, (k % KC) * P:(k % KC + 1) * P],
                                     ident[:, :])
                i.then_inc(m2_turned, 1)
                n = c.info
                lend("T", hx_lo, lambda t: NC * (t - 1) + n + 1)

            def mix2(c):
                pe.wait_ge(hx_lo, NC * c.b + c.info + 1)
                if c.info % 2 == 0:
                    take(c.slot, c.t)
                product(psA[c.slot][:, c.info % 2, 0:FA],
                        [(hx[0][:, k, :], hx[1][:, k, :], wo[0][:, k, :], wo[1][:, k, :]) for k in range(OC)]).then_inc(m2_done, 1)
                n = c.info
                lend(c.slot, m2_read, lambda t: 2 * (t - 1) + n // 2 + 1)

            def turn_out(c):
                pe.wait_ge(elu_out, c.before + (6 if not isinstance(c.t, int) or c.t < B else 2))
                take("T", c.t)
                for k in range(KC):
                    for n in range(NC):
                        i = pe.transpose(psT[:, k, n * P:(n + 1) * P], wk[:, n, k * P:(k + 1) * P], ident[:, :])
                i.then_inc(o_turned, 1)
                lend("T", oT_ready, lambda t: t)

            outT = ff[:, 0, :, :].rearrange("p c f -> p (c f)").rearrange("p (k n) -> p k n", k=KC)
            midT = ff[:, 1, :, :].rearrange("p c f -> p (c f)").rearrange("p (k n) -> p k n", k=KC)

            def ffn1(c):
                pe.wait_ge(oT_ready, c.b + 1)
                take(c.slot, c.t)
                for o in range(KC):
                    for k in range(KC):
                        i = pe.matmul(psA[c.slot][:, o, :], w1_sb[:, k, o * P:(o + 1) * P], outT[:, k, :], start=(k == 0), stop=(k == KC - 1))
                    i.then_inc(f1_done, 1)
                lend(c.slot, f1_read, lambda t: KC * t)

            def ffn2(c):
                pe.wait_ge(f1_read, KC * (c.b + 1))
                take(c.slot, c.t)
                for n in range(NC):
                    for k in range(KC):
                        i = pe.matmul(psA[c.slot][:, n // 2, (n % 2) * F:(n % 2 + 1) * F], midT[:, k, n * P:(n + 1) * P], w2_sb[:, k, :],
                                      start=(k == 0), stop=(k == KC - 1))
                i.then_inc(f2_done, 1)
                lend(c.slot, y_ready, lambda t: t)

            def turn_gc(c):
                pe.wait_ge(ln_out["gc"], c.b + 1)
                take("T", c.t)
                for k in range(KC):
                    for n in range(NC):
                        i = pe.transpose(psT[:, k, n * P:(n + 1) * P], ff[:, 1, n, k * P:(k + 1) * P], ident[:, :])
                i.then_inc(h2_turned, 1)
                lend("T", h2_lo, lambda t: t)

            def conv_in_(c):
                pe.wait_ge(h2_lo, c.b + 1)
                take(c.slot, c.t)
                for i in range(2):
                    n = 2 * c.info + i
                    r = product(psA[c.slot][:, i, :],
                                [(hx[0][:, k * NC + n, :], hx[1][:, k * NC + n, :], wg[0][:, k, :], wg[1][:, k, :]) for k in range(KC)])
                r.then_inc(conv_in, 1)
                p = c.info
                lend(c.slot, conv_in_read, lambda t: 2 * (t - 1) + p + 1)

            def conv(c):
                pe.wait_ge(mj_lo, 2 * (c.b + 1))
                take("T", c.t)
                for n in range(NC):
                    for j in range(NC):
                        for s, mj in enumerate((w2x[:, j, 0:F], w2l[:, j, :])):
                            i = pe.matmul(psT[:, n // 2, (n % 2) * F:(n % 2 + 1) * F], adjT[:, j, n * P:(n + 1) * P], mj,
                                          start=(j == 0 and s == 0), stop=(j == NC - 1 and s == 1))
                i.then_inc(conv_done, 1)
                lend("T", res_ready, lambda t: t)

            run_all(pe, {"turn_in": turn_in, "m1": m1, "f2rows": f2rows, "rowmax": rowmax, "rows": rows, "spread": spread_,
                         "attend": attend, "turn2": turn2, "mix2": mix2, "turn_out": turn_out, "ffn1": ffn1, "ffn2": ffn2,
                         "turn_gc": turn_gc, "conv_in": conv_in_, "conv": conv}, at_trip_end)


_INS = ["x", "adj", "L0_gnn_W_heads", "L0_gnn_a_heads", "L0_gnn_W_out", "L0_gnn_a_out", "L0_gnn_w1", "L0_gnn_b1",
        "L0_gnn_w2", "L0_gnn_b2", "L0_gnn_ln_gamma", "L0_gnn_ln_beta", "L1_gnn_W", "L1_gnn_b"]


def kernel(**inputs):
    import numpy as _np
    import concourse.bacc as _bacc
    from concourse import mybir as _mybir
    from concourse.bass_utils import run_bass_kernel_spmd as _run

    nc = _bacc.Bacc("TRN2", target_bir_lowering=False, num_devices=1)
    arrays, args = {}, []
    for name in _INS:
        a = _np.ascontiguousarray(inputs[name])
        arrays[f"in_{name}"] = a
        args.append(nc.dram_tensor(f"in_{name}", a.shape, _mybir.dt.from_np(a.dtype), kind="ExternalInput").ap())
    shape = arrays["in_x"].shape
    out = nc.dram_tensor("out_x", shape, _mybir.dt.float32, kind="ExternalOutput").ap()
    gnn_kernel(nc, *args, out)
    r = _run(nc, [arrays], core_ids=[0])
    return r.results[0]["out_x"]
```

```python
from contextlib import ExitStack

import concourse.bass as bass
from concourse import mybir



SP_STEPS = [
    ("load", 0, 0), ("conv", 0, 1), ("load_back", 0, 0),
]
PE_STEPS = [
    ("turn2", 2, 1), ("attend", 2, 1), ("turn2", 3, 1), ("mix2", 2, 1), ("m1", (3, 1), 1), ("turn_in", 0, 1), ("mix2", 3, 1),
    ("f2rows", 2, 1), ("rowmax", 2, 1), ("attend", 3, 1), ("rows", 2, 1), ("spread", 4, 1), ("f2rows", 1, 1), ("rowmax", 1, 1),
    ("m1", (0, 0), 1), ("m1", (0, 1), 1), ("rows", 1, 1), ("spread", 6, 1), ("attend", 4, 1), ("attend", 5, 1),
    ("m1", (1, 0), 1), ("m1", (1, 1), 1), ("spread", 8, 1), ("turn_out", 0, 1), ("attend", 6, 1), ("f2rows", 0, 1),
    ("ffn1", 0, 1), ("rowmax", 0, 1), ("attend", 7, 1), ("ffn2", 0, 1), ("rows", 0, 1), ("spread", 0, 0), ("attend", 8, 1),
    ("attend", 9, 1), ("m1", (2, 0), 0), ("spread", 2, 0), ("m1", (2, 1), 0), ("attend", 0, 0), ("turn_gc", 0, 1),
    ("attend", 1, 0), ("turn2", 0, 0), ("conv_in", 0, 1), ("m1", (3, 0), 0), ("turn2", 1, 0), ("mix2", 0, 0), ("conv_in", 1, 1),
    ("mix2", 1, 0), ("conv", 0, 1),
]
ACT_STEPS = [
    ("turn2", 2, 1), ("probs", 3, 1), ("elu_in", 2, 1), ("turn2", 3, 1), ("elu_out", 1, 1), ("m1", (3, 1), 1),
    ("turn_in", 0, 1), ("mix2", 1, 1), ("f2rows", 2, 1), ("rows", 2, 1), ("args", 4, 1), ("args", 5, 1), ("f2rows", 1, 1),
    ("elu_out", 2, 1), ("probs", 4, 1), ("m1", (0, 0), 1), ("elu_in", 3, 1), ("probs", 5, 1), ("m1", (0, 1), 1), ("rows", 1, 1),
    ("args", 6, 1), ("args", 7, 1), ("elu_in", 4, 1), ("elu_out", 3, 1), ("probs", 6, 1), ("elu_out", 4, 1), ("elu_in", 5, 1),
    ("elu_out", 5, 1), ("m1", (1, 0), 1), ("probs", 7, 1), ("m1", (1, 1), 1), ("turn_out", 0, 1), ("args", 8, 1),
    ("args", 9, 1), ("f2rows", 0, 1), ("elu_in", 6, 1), ("probs", 8, 1), ("ffn1", 0, 1), ("probs", 9, 1), ("elu_out", 6, 1),
    ("rows", 0, 1), ("elu_in", 7, 1), ("args", 0, 0), ("args", 1, 0), ("norm_ff_out", 0, 1), ("elu_out", 7, 1),
    ("elu_in", 8, 1), ("probs", 0, 0), ("elu_in", 9, 1), ("m1", (2, 0), 0), ("elu_out", 8, 1), ("probs", 1, 0),
    ("m1", (2, 1), 0), ("norm_gc_out", 0, 1), ("elu_out", 9, 1), ("turn_gc", 0, 1), ("args", 2, 0), ("elu_in", 0, 0),
    ("args", 3, 0), ("turn2", 0, 0), ("elu_in", 1, 0), ("conv_in", 0, 1), ("probs", 2, 0), ("m1", (3, 0), 0), ("turn2", 1, 0),
    ("conv_in", 1, 1), ("norm_in_out", 0, 0), ("mix2", 0, 0), ("elu_out", 0, 0),
]
DVE_STEPS = [
    ("mix2", 0, 1), ("turn2", 2, 1), ("elu_out", 0, 1), ("elu_neg", 1, 1), ("elu_in", 2, 1), ("turn2", 3, 1), ("elu_out", 1, 1),
    ("elu_neg", 2, 1), ("m1", (3, 1), 1), ("turn_in", 0, 1), ("f2rows", 1, 1), ("mix2", 1, 1), ("f2rows", 2, 1),
    ("rowmax", 2, 1), ("norm_in", 0, 0), ("args", 4, 1), ("args", 5, 1), ("elu_in", 3, 1), ("rowmax", 1, 1), ("m1", (0, 0), 1),
    ("elu_out", 2, 1), ("m1", (0, 1), 1), ("args", 6, 1), ("elu_neg", 3, 1), ("elu_in", 4, 1), ("args", 7, 1),
    ("elu_out", 3, 1), ("elu_neg", 4, 1), ("elu_in", 5, 1), ("elu_out", 4, 1), ("elu_neg", 5, 1), ("elu_out", 5, 1),
    ("m1", (1, 0), 1), ("m1", (1, 1), 1), ("f2rows", 0, 1), ("args", 8, 1), ("elu_in", 6, 1), ("args", 9, 1), ("rowmax", 0, 1),
    ("elu_neg", 6, 1), ("elu_in", 7, 1), ("ffn2", 0, 1), ("norm_ff", 0, 1), ("args", 0, 0), ("norm_ff_out", 0, 1),
    ("elu_out", 6, 1), ("elu_neg", 7, 1), ("elu_in", 8, 1), ("args", 1, 0), ("elu_out", 7, 1), ("elu_neg", 8, 1),
    ("elu_in", 9, 1), ("x2", 0, 1), ("norm_gc", 0, 1), ("m1", (2, 0), 0), ("elu_out", 8, 1), ("norm_gc_out", 0, 1),
    ("elu_neg", 9, 1), ("m1", (2, 1), 0), ("elu_out", 9, 1), ("turn_gc", 0, 1), ("elu_in", 0, 0), ("args", 2, 0),
    ("elu_neg", 0, 0), ("elu_in", 1, 0), ("turn2", 0, 0), ("norm_in_out", 0, 0), ("conv_in", 0, 1), ("args", 3, 0),
    ("m1", (3, 0), 0), ("turn2", 1, 0), ("conv_in", 1, 1), ("conv", 0, 1),
]
POOL_STEPS = [
    ("x_beta", 0, 1), ("probs", 3, 1), ("args", 4, 1), ("args", 5, 1), ("probs", 4, 1), ("probs", 5, 1), ("args", 6, 1),
    ("args", 7, 1), ("probs", 6, 1), ("probs", 7, 1), ("args", 8, 1), ("args", 9, 1), ("norm_in", 0, 0), ("probs", 8, 1),
    ("probs", 9, 1), ("norm_ff", 0, 1), ("args", 0, 0), ("gamma", 0, 1), ("args", 1, 0), ("probs", 0, 0), ("norm_gc", 0, 1),
    ("probs", 1, 0), ("args", 2, 0), ("args", 3, 0), ("probs", 2, 0),
]


def gnn_kernel(nc, x, adj, W_heads, a_heads, W_out, a_out, w1, b1, w2, b2, gamma, beta, W_gc, b_gc, out):
    fp32, f32r, bf16, i32 = mybir.dt.float32, mybir.dt.float32r, mybir.dt.bfloat16, mybir.dt.int32
    ALU = mybir.AluOpType
    ACT = mybir.ActivationFunctionType
    AX = mybir.AxisListType

    P = 128
    B, N, F = x.shape
    H = W_heads.shape[0]
    NC = N // P
    KC = F // P
    OC = H * KC
    HN = N // 2
    FA = F + 2
    UN = 2 * H
    SLOPE = 0.01
    EPS = 1e-5
    BIG = 2.0 ** 100

    x_v = x.rearrange("b (c p) f -> b p c f", p=P)
    out_v = out.rearrange("b (c p) f -> b p c f", p=P)

    ctx = ExitStack()
    with ctx:
        def sb(name, shape, dt=fp32):
            return ctx.enter_context(nc.sbuf_tensor(name, shape, dt))

        def sem(name):
            return ctx.enter_context(nc.semaphore(name))

        wh = [sb(f"wh_{s}", [P, KC, H, FA], f32r) for s in ("hi", "lo")]
        wo = [sb(f"wo_{s}", [P, OC, FA], f32r) for s in ("hi", "lo")]
        w1_sb = sb("w1_sb", [P, KC, F])
        w2_sb = sb("w2_sb", [P, KC, F])
        wg = [sb(f"wg_{s}", [P, KC, 2 * F], f32r) for s in ("hi", "lo")]
        adjT = sb("adjT", [P, NC, N], f32r)
        maskT = sb("maskT", [P, NC, N], bf16)
        mask = sb("mask", [P, NC, N], bf16)
        deg = sb("deg", [P, NC])
        brow = sb("brow", [P, F], f32r)
        ident = sb("ident", [P, P])
        b1c = sb("b1c", [P, KC])
        gamma_bc = sb("gamma_bc", [P, F])
        beta_bc = sb("beta_bc", [P, F])
        pick = sb("pick", [P, 4, P], f32r)
        mhalf = sb("mhalf", [P, NC])

        xin = sb("xin", [P, NC, F])
        hT = [sb(f"hT_{s}", [P, KC, N], f32r) for s in ("hi", "lo")]
        whx = sb("whx_hi", [P, NC, H, FA], f32r)
        whl = sb("whx_lo", [P, NC, H, F], f32r)
        w2x = sb("w2x_hi", [P, NC, FA], f32r)
        w2l = sb("w2x_lo", [P, NC, F], f32r)
        arg = sb("arg", [P, 2, NC, HN])
        prob = [sb(f"prob_{s}", [P, 2, NC, HN], f32r) for s in ("hi", "lo")]
        elu_in = sb("elu_in", [P, 2, 2, F])
        elu_ex = sb("elu_ex", [P, 2, F])
        hcat = sb("hcat", [P, NC, H, F])
        hx = [sb(f"hx_{s}", [P, 8, P], f32r) for s in ("hi", "lo")]
        ff = sb("ff", [P, 2, NC, F])
        h2T = [sb(f"h2T_{s}", [P, KC, N], f32r) for s in ("hi", "lo")]
        wk = sb("wk", [P, NC, F])
        xb = sb("xb", [P, NC, F])
        junk = sb("junk", [P, 2, N], bf16)
        held = sb("held", [P, 1])
        fcol = sb("fcol", [P, NC, H, 2])
        fcol2 = sb("fcol2", [P, NC, 1, 2])
        fs = sb("fs", [P, NC, H])
        fs2 = sb("fs2", [P, NC, 1])
        c1 = [sb(f"c1_{q}", [P, NC, 2, 2]) for q in range(3)]
        c2 = [sb(f"c2_{q}", [P, NC, 4, 2]) for q in range(3)]
        gmax = [sb(f"gmax_{q}", [P, NC, 2]) for q in range(3)]
        zrow = [sb(f"zrow_{q}", [P, 4, NC, 2]) for q in range(3)]
        f2row = sb("f2row", [P, N], f32r)
        rrow = [sb(f"rrow_{q}", [P, N], f32r) for q in range(3)]
        rec = sb("rec", [P, 2, 2])
        st = sb("st", [P, NC, 6])
        NORMS = ("in", "ff", "gc")
        mv = {k: sb(f"mv_{k}", [P, NC, 2]) for k in NORMS}
        ve = {k: sb(f"ve_{k}", [P, NC]) for k in NORMS}
        rstd = {k: sb(f"rstd_{k}", [P, NC]) for k in NORMS}
        shift = {k: sb(f"shift_{k}", [P, NC]) for k in NORMS}

        pick_st = elu_in[:, :, :, :].rearrange("p a c f -> p (a c f)").rearrange("p (w h m) -> p w h m", w=2, h=2, m=2 * P)[:, :, :, 0:P]
        identb = elu_ex[:, 1, 0:P // 2].bitcast(bf16)
        cnt, lone = elu_ex[:, 0, 0:NC], elu_ex[:, 0, NC:2 * NC]
        wsum = elu_ex[:, 0, 0:2 * OC].rearrange("p (k h s) -> p k h s", k=KC, h=H)
        wsum2 = elu_ex[:, 0, 2 * OC:4 * OC].rearrange("p (k s) -> p k s", k=OC)
        psA = [ctx.enter_context(nc.psum_tensor(f"psA{i}", [P, 2, 512], fp32)) for i in range(2)]
        psT = ctx.enter_context(nc.psum_tensor("psT", [P, 2, 512], fp32))
        psR = ctx.enter_context(nc.psum_tensor("psR", [P, 2, 512], fp32))

        NLOAD = 14
        ld = [sem(f"ld{i}") for i in range(NLOAD)]
        LD_ADJ, LD_WH, LD_A, LD_WO, LD_AO, LD_GC, LD_W1, LD_W2, LD_B1, LD_B2, LD_G, LD_BE, LD_BG, LD_A2 = range(NLOAD)
        s_zeroed = sem("s_zeroed")
        s_const = sem("s_const")
        s_picked = sem("s_picked")
        s_adj = sem("s_adj")
        s_adj_turned = sem("s_adj_turned")
        s_adj_out = sem("s_adj_out")
        s_gc_turned = sem("s_gc_turned")
        s_gc_hi = sem("s_gc_hi")
        s_setup = sem("s_setup")
        s_hi = sem("s_hi")
        s_dve = sem("s_dve")

        x_loaded = sem("x_loaded")
        ln_stat = {k: sem(f"ln_stat_{k}") for k in NORMS}
        ln_aggr = {k: sem(f"ln_aggr_{k}") for k in NORMS}
        ln_var = {k: sem(f"ln_var_{k}") for k in NORMS}
        ln_rstd = {k: sem(f"ln_rstd_{k}") for k in NORMS}
        ln_shift = {k: sem(f"ln_shift_{k}") for k in NORMS}
        ln_out = {k: sem(f"ln_out_{k}") for k in NORMS}
        h_turned = sem("h_turned")
        hT_hi = sem("hT_hi_ready")
        hT_lo = sem("hT_lo_ready")
        m1_done = sem("m1_done")
        m1_hi = sem("m1_hi")
        m1_lo = sem("m1_lo")
        m1_read = sem("m1_read")
        c1_made = [sem(f"c1_made{q}") for q in range(3)]
        c1_turned = [sem(f"c1_turned{q}") for q in range(3)]
        f2row_made = [sem(f"f2row_made{q}") for q in range(3)]
        f2_spread = [sem(f"f2_spread{q}") for q in range(3)]
        max_made = [sem(f"max_made{q}") for q in range(3)]
        row_math = [sem(f"row_math{q}") for q in range(3)]
        c2_turned = [sem(f"c2_turned{q}") for q in range(3)]
        rrow_made = [sem(f"rrow_made{q}") for q in range(3)]
        m2_turned = sem("m2_turned")
        hx_hi = sem("hx_hi_ready")
        hx_lo = sem("hx_lo_ready")
        m2_done = sem("m2_done")
        m2_hi = sem("m2_hi")
        m2_lo = sem("m2_lo")
        m2_read = sem("m2_read")
        xb_loaded = sem("xb_loaded")
        o_turned = sem("o_turned")
        oT_ready = sem("oT_ready")
        x_beta = sem("x_beta")
        f1_done = sem("f1_done")
        f1_read = sem("f1_read")
        f2_done = sem("f2_done")
        y_ready = sem("y_ready")
        y_gamma = sem("y_gamma")
        x2_ready = sem("x2_ready")
        h2_turned = sem("h2_turned")
        h2_hi = sem("h2_hi")
        h2_lo = sem("h2_lo")
        conv_in = sem("conv_in")
        mj_hi = sem("mj_hi")
        mj_lo = sem("mj_lo")
        conv_in_read = sem("conv_in_read")
        conv_done = sem("conv_done")
        res_ready = sem("res_ready")
        stored = sem("stored")

        spread = sem("spread")
        arg_lin = sem("arg_lin")
        arg_max = sem("arg_max")
        arg_masked = sem("arg_masked")
        prob_hi = sem("prob_hi")
        prob_exp = sem("prob_exp")
        prob_lo = sem("prob_lo")
        att_done = sem("att_done")
        elu_rec = sem("elu_rec")
        elu_x = sem("elu_x")
        elu_neg = sem("elu_neg")
        elu_exp = sem("elu_exp")
        elu_out = sem("elu_out")

        block = ctx.enter_context(nc.Block())

        def wait(eng, s, count):
            if not isinstance(count, int) or count > 0:
                eng.wait_ge(s, count)

        BACK = -1
        UNITS = [(0, 0), (0, 1), (1, 0), (1, 1), (BACK, 0), (BACK, 1), (2, 0), (2, 1), (3, 0), (3, 1)]
        UNIT_STEPS = ("spread", "args", "probs", "attend", "elu_in", "elu_neg", "elu_out")
        IN_PSA = ("m1", "attend", "mix2", "ffn1", "ffn2", "conv_in")

        def batch_of(name, info, r):
            if name in UNIT_STEPS:
                return r - 1 if UNITS[info][0] == BACK else r
            if name == "m1":
                return r if info[0] >= 2 else r + 1
            if name in ("f2rows", "rowmax", "rows"):
                return (r + 1, r, r - 1)[info]
            return r + 1 if name in ("load", "norm_in", "norm_in_out", "turn_in") else r - 1

        def units_before(r):
            return 0 if isinstance(r, int) and r <= 0 else (UN + 2) * r - 2

        def unit_number(r, s):
            if isinstance(r, int) and (r == 0 and s >= 4 or r == B):
                s = s - 2 if r == 0 else s - 4
            return units_before(r) + s

        def psa_pairs():
            users = []
            for name, info, _ in PE_STEPS:
                key = (name, info // 2 if name == "mix2" else info)
                if name in IN_PSA and key not in users:
                    users.append(key)
            assert len(users) % 2 == 0
            return {key: k % 2 for k, key in enumerate(users)}

        pair_of = psa_pairs()

        class Step:
            pass

        def run_all(eng, table, steps_of, at_trip_end=lambda: None):
            def trip(t):
                for name, info, late in table:
                    c = Step()
                    c.r, c.late, c.info = t - late, late, info
                    c.b = batch_of(name, info, c.r)
                    if isinstance(c.b, int) and not 0 <= c.b < B:
                        continue
                    c.before = units_before(c.r)
                    if name in UNIT_STEPS:
                        c.h, c.u = UNITS[info]
                        c.unit, c.buf = unit_number(c.r, info), info % 2
                    c.pair = pair_of.get(("attend" if name == "elu_in" else name,
                                          info // 2 if name == "mix2" and table is PE_STEPS else info))
                    steps_of[name](c)
                at_trip_end()

            LATE = 1
            for t in range(-1, 2 + LATE):
                trip(t)
            with eng.Fori(2 + LATE, B - 1) as t:
                trip(t)
            for t in range(B - 1, B + 1 + LATE):
                trip(t)

        def heads_of(q):
            return (0, 2) if q == 0 else (2, 2) if q == 1 else (0, 1)

        @block.sync
        def _(sp):
            sp.dma_start(arg[:, :, :, :].rearrange("p a c n -> p (a c n)").bitcast(i32).rearrange("p (c n) -> p c n", c=NC),
                         adj.rearrange("(c p) n -> p c n", p=P)).then_inc(ld[LD_ADJ], 16)
            sp.dma_start(xb[:, :, :].rearrange("p (a c) f -> p a (c f)", a=2), W_gc.rearrange("(a p) d -> p a d", p=P)).then_inc(ld[LD_GC], 16)
            for k in range(KC):
                sp.dma_start(hcat[:, k, :, :], W_heads[:, k * P:(k + 1) * P, :].rearrange("h p o -> p h o")).then_inc(ld[LD_WH], 16)
            sp.dma_start(ff[:, :, :, :].rearrange("p a c f -> p (a c f)").rearrange("p (h f) -> p h f", h=H),
                         a_heads.partition_broadcast(P)).then_inc(ld[LD_A], 16)
            sp.dma_start(hcat[:, KC:NC, :, :].rearrange("p a h f -> p (a h) f"), W_out.rearrange("(k p) o -> p k o", p=P)).then_inc(ld[LD_WO], 16)
            sp.dma_start(wk[:, 0:2, :].rearrange("p c f -> p (c f)"), a_out.partition_broadcast(P)).then_inc(ld[LD_AO], 16)
            sp.dma_start(wk[:, 2, :], b_gc.partition_broadcast(P)).then_inc(ld[LD_BG], 16)
            sp.dma_start(w1_sb[:, :, :], w1.rearrange("(k p) o -> p k o", p=P)).then_inc(ld[LD_W1], 16)
            sp.dma_start(w2_sb[:, :, :], w2.rearrange("(k p) o -> p k o", p=P)).then_inc(ld[LD_W2], 16)
            sp.dma_start(b1c[:, :], b1.rearrange("(k p) -> p k", p=P), allow_slow_non_contiguous=True).then_inc(ld[LD_B1], 16)
            sp.dma_start(wk[:, 3, :], b2.partition_broadcast(P)).then_inc(ld[LD_B2], 16)
            sp.dma_start(gamma_bc[:, :], gamma.partition_broadcast(P)).then_inc(ld[LD_G], 16)
            sp.dma_start(beta_bc[:, :], beta.partition_broadcast(P)).then_inc(ld[LD_BE], 16)

            def load(c):
                wait(sp, h_turned, c.b)
                sp.dma_start(xin[:, :, :], x_v[c.b]).then_inc(x_loaded, 16)

            def load_back(c):
                wait(sp, s_setup, 1)
                wait(sp, stored, 16 * c.b)
                sp.dma_start(xb[:, :, :], x_v[c.b]).then_inc(xb_loaded, 16)

            def conv(c):
                wait(sp, res_ready, c.b + 1)
                sp.dma_start(out_v[c.b], xb[:, :, :]).then_inc(stored, 16)

            run_all(sp, SP_STEPS, {"load": load, "load_back": load_back, "conv": conv})
            sp.wait_ge(stored, 16 * B)

        @block.gpsimd
        def _(pool):
            pool.memset(ident[:, :], 0.0).then_inc(s_zeroed, 1)
            pool.memset(mhalf[:, :], -0.5).then_inc(s_zeroed, 1)
            pool.memset(pick_st, 0.0).then_inc(s_zeroed, 1)
            pool.wait_ge(s_zeroed, 3)
            pool.affine_select(out=ident[:, :], in_=ident[:, :], compare_op=ALU.not_equal, fill=1.0, base=0,
                               pattern=[[-1, P]], channel_multiplier=1).then_inc(s_const, 1)
            for z in range(2):
                pool.affine_select(out=pick_st, in_=pick_st, compare_op=ALU.not_equal, fill=1.0, base=-2 * z,
                                   pattern=[[-4, 2], [-1, 2], [0, P]], channel_multiplier=1).then_inc(s_const, 1)
                pool.wait_ge(s_const, 2 + z)

            def norm(k):
                def step(c):
                    pool.wait_ge(ln_var[k], c.b + 1)
                    pool.tensor_tensor(out=rstd[k][:, :], in0=ve[k][:, :], in1=mhalf[:, :], op=ALU.pow).then_inc(ln_rstd[k], 1)
                return step

            def args(c):
                pool.wait_ge(arg_max, NC * (c.unit + 1))
                a = arg[:, c.buf, :, :]
                pool.tensor_tensor(out=a, in0=a, in1=maskT[:, :, c.u * HN:(c.u + 1) * HN], op=ALU.add).then_inc(arg_masked, 1)

            def probs(c):
                pool.wait_ge(prob_exp, c.unit + 1)
                pool.tensor_tensor(out=prob[1][:, c.buf, :, :], in0=arg[:, c.buf, :, :], in1=prob[0][:, c.buf, :, :].bitcast(fp32),
                                   op=ALU.subtract).then_inc(prob_lo, 1)

            def x_beta_(c):
                pool.wait_ge(xb_loaded, 16 * (c.b + 1))
                pool.tensor_tensor(out=xb[:, :, :], in0=xb[:, :, :], in1=beta_bc[:, None, :].to_broadcast([P, NC, F]),
                                   op=ALU.add).then_inc(x_beta, 1)

            def gamma_(c):
                pool.wait_ge(ln_out["ff"], c.b + 1)
                pool.tensor_tensor(out=wk[:, :, :], in0=wk[:, :, :], in1=gamma_bc[:, None, :].to_broadcast([P, NC, F]),
                                   op=ALU.mult).then_inc(y_gamma, 1)

            for l in (LD_G, LD_BE):
                pool.wait_ge(ld[l], 16)
            pool.wait_ge(s_setup, 1)
            run_all(pool, POOL_STEPS, {"norm_in": norm("in"), "args": args, "probs": probs, "x_beta": x_beta_,
                                       "norm_ff": norm("ff"), "gamma": gamma_, "norm_gc": norm("gc")})

        @block.scalar
        def _(act):
            act.wait_ge(ld[LD_WH], 16 * KC)
            act.activation(wh[0][:, :, :, 0:F], hcat[:, 0:KC, :, :], ACT.Copy).then_inc(s_hi, 1)
            act.wait_ge(ld[LD_WO], 16)
            act.activation(wo[0][:, :, 0:F], hcat[:, KC:NC, :, :].rearrange("p a h f -> p (a h) f"), ACT.Copy).then_inc(s_hi, 1)
            act.wait_ge(s_gc_turned, 1)
            act.activation(wg[0][:, :, :], psR[:, :, :], ACT.Copy).then_inc(s_gc_hi, 1)
            act.wait_ge(ld[LD_B1], 16)
            act.wait_ge(s_setup, 1)

            def norm_out(k, src, dst, func):
                def step(c):
                    act.wait_ge(ln_shift[k], c.b + 1)
                    for n in range(NC):
                        i = act.activation(dst[:, n, :], src[:, n, :], func, bias=shift[k][:, n:n + 1],
                                           scale=rstd[k][:, n:n + 1])
                    i.then_inc(ln_out[k], 1)
                return step

            def turn_in(c):
                act.wait_ge(h_turned, c.b + 1)
                wait(act, m1_done, 2 * H * c.b)
                act.activation(hT[0][:, :, :], psT[:, :, :], ACT.Copy).then_inc(hT_hi, 1)

            def m1(c):
                h, p = c.info
                act.wait_ge(m1_done, 2 * H * c.b + 2 * h + p + 1)
                if not isinstance(c.b, int) or c.b > 0:
                    wait(act, att_done, c.before + (2 * h + 2 if h < 2 else -2 if h == 2 else 0))
                act.activation(whx[:, 2 * p:2 * p + 2, h, 0:F], psA[c.pair][:, :, 0:F], ACT.Copy).then_inc(m1_hi, 1)

            def f2rows(c):
                q = c.info
                act.wait_ge(c1_turned[q], c.b + 1)
                act.activation(f2row[0:4, :], psT[0:4, 0, :], ACT.Copy).then_inc(f2row_made[q], 1)

            def rows(c):
                q = c.info
                act.wait_ge(c2_turned[q], c.b + 1)
                if not isinstance(c.b, int) or c.b > 0:
                    wait(act, spread, c.before + (4, 0, -4)[q])
                act.activation(rrow[q][0:8, :], psT[0:8, 0, :], ACT.Copy).then_inc(rrow_made[q], 1)

            def args(c):
                act.wait_ge(spread, c.unit - c.u + 2)
                wait(act, prob_lo, c.unit - 1)
                f = fs2[:, :, 0] if c.h == BACK else fs[:, :, c.h]
                for j in range(NC):
                    act.activation(arg[:, c.buf, j, :], psR[:, 1, c.u * HN:(c.u + 1) * HN], ACT.Identity,
                                   bias=f[:, j:j + 1]).then_inc(arg_lin, 1)

            def probs(c):
                act.wait_ge(arg_masked, c.unit + 1)
                wait(act, att_done, c.unit - 1)
                act.activation(prob[0][:, c.buf, :, :], arg[:, c.buf, :, :], ACT.Exp).then_inc(prob_hi, 1)
                act.activation(arg[:, c.buf, :, :], arg[:, c.buf, :, :], ACT.Exp).then_inc(prob_exp, 1)

            def elu_in_(c):
                act.wait_ge(elu_rec, c.unit + 1)
                wait(act, elu_out, c.unit - 1)
                for n in range(2):
                    i = act.activation(elu_in[:, c.buf, n, :], psA[c.pair][:, n, 0:F], ACT.Copy,
                                       scale=rec[:, c.buf, n:n + 1])
                i.then_inc(elu_x, 1)

            def elu_out_(c):
                act.wait_ge(elu_neg, c.unit + 1)
                act.activation(elu_ex[:, :, :], elu_ex[:, :, :], ACT.Exp).then_inc(elu_exp, 1)

            def turn2(c):
                act.wait_ge(m2_turned, NC * c.b + c.info + 1)
                wait(act, m2_done, NC * c.b + c.info)
                act.activation(hx[0][:, :, :], psT[:, :, :].rearrange("p a n -> p (a n)").rearrange("p (k n) -> p k n", k=OC),
                               ACT.Copy).then_inc(hx_hi, 1)

            def mix2(c):
                act.wait_ge(m2_done, NC * c.b + 2 * c.info + 2)
                wait(act, conv_done, c.b)
                act.activation(w2x[:, 2 * c.info:2 * c.info + 2, 0:F], psA[c.pair][:, :, 0:F], ACT.Copy).then_inc(m2_hi, 1)

            def turn_out(c):
                act.wait_ge(o_turned, c.b + 1)
                act.activation(ff[:, 0, :, :], psT[:, :, :].rearrange("p a n -> p (a n)").rearrange("p (k n) -> p k n", k=NC),
                               ACT.Copy).then_inc(oT_ready, 1)

            def ffn1(c):
                for o in range(KC):
                    act.wait_ge(f1_done, KC * c.b + o + 1)
                    act.activation(ff[:, 1, 2 * o:2 * o + 2, :].rearrange("p c f -> p (c f)"), psA[c.pair][:, o, :], ACT.Relu,
                                   bias=b1c[:, o:o + 1]).then_inc(f1_read, 1)

            def turn_gc(c):
                act.wait_ge(h2_turned, c.b + 1)
                act.activation(h2T[0][:, :, :], psT[:, :, :], ACT.Copy).then_inc(h2_hi, 1)

            def conv_in_(c):
                act.wait_ge(conv_in, 2 * c.b + c.info + 1)
                act.activation(w2x[:, 2 * c.info:2 * c.info + 2, 0:F], psA[c.pair][:, :, F:2 * F], ACT.Copy).then_inc(mj_hi, 1)

            run_all(act, ACT_STEPS, {"norm_in_out": norm_out("in", xin, xin, ACT.Relu), "turn_in": turn_in, "m1": m1, "f2rows": f2rows,
                          "rows": rows, "args": args, "probs": probs, "elu_in": elu_in_, "elu_out": elu_out_,
                          "turn2": turn2, "mix2": mix2, "turn_out": turn_out, "ffn1": ffn1,
                          "norm_ff_out": norm_out("ff", wk, wk, ACT.Identity),
                          "norm_gc_out": norm_out("gc", xb, ff[:, 1, :, :], ACT.Relu),
                          "turn_gc": turn_gc, "conv_in": conv_in_})

        @block.vector
        def _(dve):
            count = [0]

            def link(ins):
                count[0] += 1
                ins.then_inc(s_dve, 1)
                dve.wait_ge(s_dve, count[0])

            adj_f = arg[:, :, :, :].rearrange("p a c n -> p (a c n)").rearrange("p (c n) -> p c n", c=NC)
            dve.wait_ge(ld[LD_ADJ], 16)
            link(dve.tensor_copy(adj_f, adj_f.bitcast(i32)))
            dve.tensor_scalar(mask[:, :, :], adj_f, 0.0, 1.0, ALU.is_gt, ALU.mult).then_inc(s_adj, 1)
            link(dve.tensor_reduce(out=deg[:, :], in_=adj_f, axis=AX.X, op=ALU.add))
            dve.wait_ge(s_adj, 1)
            link(dve.tensor_reduce(out=cnt, in_=mask[:, :, :], axis=AX.X, op=ALU.add))
            link(dve.tensor_scalar(lone, cnt, 0.0, 2.0 * BIG, ALU.is_equal, ALU.mult))
            link(dve.tensor_scalar(lone, lone, -BIG, None, ALU.add))
            dve.wait_ge(s_const, 3)
            link(dve.tensor_copy(identb, ident[:, :]))
            for n in range(NC):
                dve.tensor_scalar(mask[:, n, :], mask[:, n, :], BIG, lone[:, n:n + 1], ALU.mult, ALU.add).then_inc(s_adj, 1)
            link(dve.tensor_copy(pick[:, :, :].rearrange("p (w h) m -> p w h m", w=2), pick_st))
            dve.memset(f2row[:, :].bitcast(fp32), 0.0)
            for q in range(3):
                dve.memset(rrow[q][:, :].bitcast(fp32), 0.0)
                dve.memset(c1[q][:, :, :, :], 0.0)
                dve.memset(c2[q][:, :, :, :], 0.0)
            dve.memset(whx[:, :, :, F:FA].bitcast(fp32), 1.0)
            link(dve.memset(w2x[:, :, F:FA].bitcast(fp32), 1.0))
            for n in range(NC):
                dve.wait_ge(s_adj_turned, n + 1)
                dve.tensor_copy(adjT[:, :, n * P:(n + 1) * P], psT[:, n % 2, :].rearrange("p (j i) -> p j i", j=NC))
                dve.tensor_copy(maskT[:, :, n * P:(n + 1) * P],
                                psA[n % 2][:, 0, 0:N // 2].bitcast(bf16).rearrange("p (j i) -> p j i", j=NC)).then_inc(s_adj_out, 1)
            dve.wait_ge(s_gc_hi, 1)
            dve.tensor_tensor(out=wg[1][:, :, :], in0=psR[:, :, :], in1=wg[0][:, :, :].bitcast(fp32), op=ALU.subtract)
            for l in (LD_BG, LD_B2):
                dve.wait_ge(ld[l], 16)
            for k in range(2):
                link(dve.tensor_copy(w2x[:, k, 0:F], wk[:, 2 + k, :]))
                link(dve.tensor_tensor(out=elu_ex[:, k, :], in0=wk[:, 2 + k, :], in1=w2x[:, k, 0:F].bitcast(fp32), op=ALU.subtract))
                link(dve.tensor_scalar(elu_ex[:, k, :], elu_ex[:, k, :], ident[:, 2 + k:3 + k], None, ALU.mult))
                link(dve.scalar_tensor_tensor(out=elu_ex[:, k, :], in0=w2x[:, k, 0:F].bitcast(fp32), scalar=ident[:, k:k + 1],
                                              in1=elu_ex[:, k, :], op0=ALU.mult, op1=ALU.add))
            link(dve.tensor_tensor(out=brow[:, :], in0=elu_ex[:, 0, :], in1=elu_ex[:, 1, :], op=ALU.add))
            a_h = ff[:, :, :, :].rearrange("p a c f -> p (a c f)").rearrange("p (h s f) -> p h s f", h=H, s=2)
            a_o = wk[:, 0:2, :]
            w_o = hcat[:, KC:NC, :, :].rearrange("p a h f -> p (a h) f")
            dve.wait_ge(ld[LD_WH], 16 * KC)
            for l in (LD_A, LD_WO, LD_AO):
                dve.wait_ge(ld[l], 16)
            for s in range(2):
                for k in range(KC):
                    for h in range(H):
                        link(dve.tensor_tensor_reduce(out=junk[:, 0, 0:F], in0=hcat[:, k, h, :], in1=a_h[:, h, s, :], scale=1.0,
                                                      scalar=0.0, op0=ALU.mult, op1=ALU.add, accum_out=wsum[:, k, h, s:s + 1]))
                for k in range(OC):
                    link(dve.tensor_tensor_reduce(out=junk[:, 0, 0:F], in0=w_o[:, k, :], in1=a_o[:, s, :], scale=1.0,
                                                  scalar=0.0, op0=ALU.mult, op1=ALU.add, accum_out=wsum2[:, k, s:s + 1]))
            dve.tensor_copy(wh[0][:, :, :, F:FA], wsum[:, :, :, :])
            link(dve.tensor_copy(wo[0][:, :, F:FA], wsum2[:, :, :]))
            dve.wait_ge(s_hi, 2)
            for k in range(KC):
                dve.tensor_tensor(out=wh[1][:, k, :, F:FA], in0=wsum[:, k, :, :], in1=wh[0][:, k, :, F:FA].bitcast(fp32), op=ALU.subtract)
                dve.tensor_tensor(out=wh[1][:, k, :, 0:F], in0=hcat[:, k, :, :], in1=wh[0][:, k, :, 0:F].bitcast(fp32), op=ALU.subtract)
            dve.tensor_tensor(out=wo[1][:, :, F:FA], in0=wsum2[:, :, :], in1=wo[0][:, :, F:FA].bitcast(fp32), op=ALU.subtract)
            link(dve.tensor_tensor(out=wo[1][:, :, 0:F], in0=w_o, in1=wo[0][:, :, 0:F].bitcast(fp32), op=ALU.subtract))
            dve.memset(junk[:, 0, 0:2], 0.0).then_inc(s_setup, 1)

            def norm(k, src, ready, per):
                def step(c):
                    dve.wait_ge(ready, per * (c.b + 1))
                    for n in range(NC):
                        i = dve.bn_stats(st[:, n, :], src[:, n, :])
                    i.then_inc(ln_stat[k], 1)
                    dve.wait_ge(s_setup, 1)
                    dve.wait_ge(ln_stat[k], c.b + 1)
                    for n in range(NC):
                        i = dve.bn_aggr(mv[k][:, n, :], st[:, n, :])
                    i.then_inc(ln_aggr[k], 1)
                    dve.wait_ge(ln_aggr[k], c.b + 1)
                    dve.tensor_scalar(ve[k][:, :], mv[k][:, :, 1], EPS, None, ALU.add).then_inc(ln_var[k], 1)
                return step

            def norm_out(k):
                def step(c):
                    dve.wait_ge(ln_rstd[k], c.b + 1)
                    dve.scalar_tensor_tensor(out=shift[k][:, :], in0=mv[k][:, :, 0], scalar=-1.0, in1=rstd[k][:, :],
                                             op0=ALU.mult, op1=ALU.mult).then_inc(ln_shift[k], 1)
                return step

            def lo(dst, src, hi):
                return dve.tensor_tensor(out=dst, in0=src, in1=hi.bitcast(fp32), op=ALU.subtract)

            def turn_in(c):
                dve.wait_ge(hT_hi, c.b + 1)
                lo(hT[1][:, :, :], psT[:, :, :], hT[0][:, :, :]).then_inc(hT_lo, 1)

            def m1(c):
                h, p = c.info
                dve.wait_ge(m1_hi, 2 * H * c.b + 2 * h + p + 1)
                ps = psA[c.pair]
                lo(whl[:, 2 * p:2 * p + 2, h, :], ps[:, :, 0:F], whx[:, 2 * p:2 * p + 2, h, 0:F]).then_inc(m1_lo, 1)
                dve.tensor_copy(fcol[:, 2 * p:2 * p + 2, h, :], ps[:, :, F:FA]).then_inc(m1_read, 1)

            def cols(q):
                h0, nh = heads_of(q)
                return (fcol2 if q == 2 else fcol)[:, :, h0:h0 + nh, :], (fs2 if q == 2 else fs)[:, :, h0:h0 + nh], nh

            def f2rows(c):
                q = c.info
                f, f_s, nh = cols(q)
                if q == 2:
                    dve.wait_ge(m2_read, 2 * (c.b + 1))
                else:
                    dve.wait_ge(m1_read, 2 * H * c.b + 4 * q + 4)
                dve.tensor_scalar(f_s, f[:, :, :, 1], SLOPE, None, ALU.mult).then_inc(c1_made[q], 1)
                dve.tensor_copy(c1[q][:, :, 0, 0:nh].bitcast(f32r), f[:, :, :, 1]).then_inc(c1_made[q], 1)
                dve.wait_ge(c1_made[q], 3 * c.b + 2)
                dve.tensor_tensor(out=c1[q][:, :, 1, 0:nh], in0=f[:, :, :, 1], in1=c1[q][:, :, 0, 0:nh],
                                  op=ALU.subtract).then_inc(c1_made[q], 1)

            def rowmax(c):
                q = c.info
                f, _, nh = cols(q)
                dve.wait_ge(f2_spread[q], c.b + 1)
                dve.memset(held[:, :], 0.0)
                for k in range(nh * NC):
                    hh, n = k // NC, k % NC
                    if k and k % 2 == 0:
                        dve.wait_ge(max_made[q], nh * NC * c.b + k)
                        dve.memset(held[:, :], 0.0)
                    dve.tensor_tensor_reduce(out=junk[:, k % 2, :], in0=psT[:, hh, :], in1=mask[:, n, :], scale=1.0,
                                             scalar=-3.0e38, op0=ALU.add, op1=ALU.max,
                                             accum_out=gmax[q][:, n, hh:hh + 1]).then_inc(max_made[q], 1)
                dve.wait_ge(max_made[q], nh * NC * (c.b + 1))
                z, m, ra, rb = (zrow[q][:, k, :, 0:nh] for k in range(4))
                f1 = f[:, :, :, 0]
                g = gmax[q][:, :, 0:nh]
                done = row_math[q]

                def after(k):
                    dve.wait_ge(done, 8 * c.b + k)

                dve.tensor_tensor(out=z, in0=f1, in1=g, op=ALU.add).then_inc(done, 1)
                after(1)
                dve.scalar_tensor_tensor(out=m, in0=z, scalar=SLOPE, in1=z, op0=ALU.mult, op1=ALU.max).then_inc(done, 1)
                after(2)
                dve.tensor_tensor(out=ra, in0=f1, in1=m, op=ALU.subtract).then_inc(done, 1)
                dve.scalar_tensor_tensor(out=rb, in0=f1, scalar=SLOPE, in1=m, op0=ALU.mult, op1=ALU.subtract).then_inc(done, 1)
                k = [c2[q][:, :, i, 0:nh] for i in range(4)]
                after(3)
                dve.tensor_copy(k[0].bitcast(f32r), ra).then_inc(done, 1)
                after(4)
                dve.tensor_copy(k[2].bitcast(f32r), rb).then_inc(done, 1)
                after(5)
                dve.tensor_tensor(out=k[1], in0=ra, in1=k[0], op=ALU.subtract).then_inc(done, 1)
                after(6)
                dve.tensor_tensor(out=k[3], in0=rb, in1=k[2], op=ALU.subtract).then_inc(done, 1)

            def args(c):
                f = fcol2[:, :, 0, 1] if c.h == BACK else fcol[:, :, c.h, 1]
                for j in range(NC):
                    dve.wait_ge(arg_lin, NC * c.unit + j + 1)
                    a = arg[:, c.buf, j, :]
                    dve.scalar_tensor_tensor(out=a, in0=psR[:, 0, c.u * HN:(c.u + 1) * HN], scalar=f[:, j:j + 1], in1=a,
                                             op0=ALU.add, op1=ALU.max).then_inc(arg_max, 1)

            def elu_in_(c):
                dve.wait_ge(att_done, c.unit + 1)
                dve.reciprocal(rec[:, c.buf, :], psA[c.pair][:, :, F]).then_inc(elu_rec, 1)

            def elu_neg_(c):
                dve.wait_ge(elu_x, c.unit + 1)
                wait(dve, elu_out, c.unit)
                dve.tensor_scalar(elu_ex[:, :, :], elu_in[:, c.buf, :, :], 0.0, None, ALU.min).then_inc(elu_neg, 1)

            def elu_out_(c):
                dve.wait_ge(elu_exp, c.unit + 1)
                if c.h == BACK:
                    dst = wk[:, 2 * c.u:2 * c.u + 2, :]
                else:
                    wait(dve, m2_turned, NC * c.b)
                    dst = hcat[:, 2 * c.u:2 * c.u + 2, c.h, :]
                dve.scalar_tensor_tensor(out=dst, in0=elu_ex[:, :, :], scalar=-1.0, in1=elu_in[:, c.buf, :, :],
                                         op0=ALU.add, op1=ALU.max).then_inc(elu_out, 1)

            hx_of_T = psT[:, :, :].rearrange("p a n -> p (a n)").rearrange("p (k n) -> p k n", k=OC)

            def turn2(c):
                dve.wait_ge(hx_hi, NC * c.b + c.info + 1)
                lo(hx[1][:, :, :], hx_of_T, hx[0][:, :, :]).then_inc(hx_lo, 1)

            def mix2(c):
                dve.wait_ge(m2_hi, 2 * c.b + c.info + 1)
                ps, n = psA[c.pair], 2 * c.info
                lo(w2l[:, n:n + 2, :], ps[:, :, 0:F], w2x[:, n:n + 2, 0:F]).then_inc(m2_lo, 1)
                dve.tensor_copy(fcol2[:, n:n + 2, 0, :], ps[:, :, F:FA]).then_inc(m2_read, 1)

            def ffn2(c):
                dve.wait_ge(f2_done, c.b + 1)
                dve.tensor_tensor(out=wk[:, :, :], in0=psA[c.pair][:, :, :].rearrange("p a (c f) -> p (a c) f", c=2), in1=wk[:, :, :],
                                  op=ALU.add).then_inc(y_ready, 1)

            def x2(c):
                dve.wait_ge(y_gamma, c.b + 1)
                dve.wait_ge(x_beta, c.b + 1)
                dve.tensor_tensor(out=xb[:, :, :], in0=xb[:, :, :], in1=wk[:, :, :], op=ALU.add).then_inc(x2_ready, 1)

            def turn_gc(c):
                dve.wait_ge(h2_hi, c.b + 1)
                lo(h2T[1][:, :, :], psT[:, :, :], h2T[0][:, :, :]).then_inc(h2_lo, 1)

            def conv_in_(c):
                p, ps = c.info, psA[c.pair]
                dve.wait_ge(mj_hi, 2 * c.b + p + 1)
                lo(w2l[:, 2 * p:2 * p + 2, :], ps[:, :, F:2 * F], w2x[:, 2 * p:2 * p + 2, 0:F]).then_inc(mj_lo, 1)
                dve.wait_ge(ln_out["gc"], c.b + 1)
                for i in range(2):
                    n = 2 * p + i
                    r = dve.scalar_tensor_tensor(out=xb[:, n, :], in0=ps[:, i, 0:F], scalar=deg[:, n:n + 1], in1=xb[:, n, :],
                                                 op0=ALU.mult, op1=ALU.add)
                r.then_inc(conv_in_read, 1)

            def conv(c):
                dve.wait_ge(conv_done, c.b + 1)
                dve.wait_ge(conv_in_read, 2 * (c.b + 1))
                dve.tensor_tensor(out=xb[:, :, :], in0=psT[:, :, :].rearrange("p a (c f) -> p (a c) f", c=2), in1=xb[:, :, :],
                                  op=ALU.add).then_inc(res_ready, 1)

            run_all(dve, DVE_STEPS, {"norm_in": norm("in", xin, x_loaded, 16), "norm_in_out": norm_out("in"), "turn_in": turn_in, "m1": m1,
                                     "f2rows": f2rows, "rowmax": rowmax, "args": args, "elu_in": elu_in_, "elu_neg": elu_neg_,
                                     "elu_out": elu_out_, "turn2": turn2, "mix2": mix2, "ffn2": ffn2,
                                     "norm_ff": norm("ff", wk, y_ready, 1), "norm_ff_out": norm_out("ff"), "x2": x2,
                                     "norm_gc": norm("gc", xb, x2_ready, 1), "norm_gc_out": norm_out("gc"),
                                     "turn_gc": turn_gc, "conv_in": conv_in_, "conv": conv})

        @block.tensor
        def _(pe):
            adj_f = arg[:, :, :, :].rearrange("p a c n -> p (a c n)").rearrange("p (c n) -> p c n", c=NC)
            pe.wait_ge(s_const, 3)
            pe.wait_ge(s_adj, 1 + NC)
            for n in range(NC):
                wait(pe, s_adj_out, n - 1)
                for j in range(NC):
                    pe.transpose(psT[:, n % 2, j * P:(j + 1) * P], adj_f[:, n, j * P:(j + 1) * P], ident[:, :])
                    i = pe.transpose(psA[n % 2][:, 0, j * P // 2:(j + 1) * P // 2].bitcast(bf16), mask[:, n, j * P:(j + 1) * P], identb)
                i.then_inc(s_adj_turned, 1)
            pe.wait_ge(ld[LD_GC], 16)
            w_gc = xb[:, :, :].rearrange("p (a c) f -> p a (c f)", a=2)
            for k in range(KC):
                for side in range(2):
                    for o in range(KC):
                        i = pe.transpose(psR[:, k, side * F + o * P:side * F + (o + 1) * P],
                                         w_gc[:, o, side * F + k * P:side * F + (k + 1) * P], ident[:, :])
            i.then_inc(s_gc_turned, 1)
            for l in (LD_W1, LD_W2):
                pe.wait_ge(ld[l], 16)
            pe.wait_ge(s_setup, 1)

            lent = {}

            def take(ps, c):
                if ps in lent:
                    s, at, late = lent[ps]
                    wait(pe, s, at(c.r + c.late - late))

            def lend(ps, c, s, at):
                lent[ps] = (s, at, c.late)

            def at_trip_end():
                for ps, (s, at, late) in lent.items():
                    lent[ps] = (s, at, late + 1)

            def product(out, steps, wide=None, also=None):
                n = 3 * len(steps)
                k = 0
                for lh, ll, rh, rl in steps:
                    for a, b_, o in ((lh, rh, wide if wide is not None else out), (ll, rh, wide if wide is not None else out), (lh, rl, out)):
                        i = pe.matmul(o, a, b_, start=(k == 0), stop=(k == n - 1))
                        k += 1
                        if also and k == 1:
                            pe.matmul(*also, start=False, stop=False)
                return i

            def turn_in(c):
                pe.wait_ge(ln_out["in"], c.b + 1)
                take("T", c)
                for k in range(KC):
                    for n in range(NC):
                        i = pe.transpose(psT[:, k, n * P:(n + 1) * P], xin[:, n, k * P:(k + 1) * P], ident[:, :])
                i.then_inc(h_turned, 1)
                lend("T", c, hT_lo, lambda r: r + 2)

            def m1(c):
                h, p = c.info
                pe.wait_ge(hT_lo, c.b + 1)
                take(c.pair, c)
                for i in range(2):
                    n = 2 * p + i
                    r = product(psA[c.pair][:, i, 0:FA],
                                [(hT[0][:, k, n * P:(n + 1) * P], hT[1][:, k, n * P:(n + 1) * P], wh[0][:, k, h, :], wh[1][:, k, h, :])
                                 for k in range(KC)])
                r.then_inc(m1_done, 1)
                off = 1 if h < 2 else 0
                lend(c.pair, c, m1_read, lambda r: 2 * H * (r + off) + 2 * h + p + 1)

            def f2rows(c):
                q = c.info
                pe.wait_ge(c1_made[q], 3 * (c.b + 1))
                take("T", c)
                for n in range(NC):
                    i = pe.transpose(psT[0:4, 0, n * P:(n + 1) * P], c1[q][:, n, :, :].rearrange("p a h -> p (a h)"), ident[:, :])
                i.then_inc(c1_turned[q], 1)
                off = (1, 0, -1)[q]
                lend("T", c, f2row_made[q], lambda r: r + off + 1)

            def rowmax(c):
                q = c.info
                nh = heads_of(q)[1]
                pe.wait_ge(f2row_made[q], c.b + 1)
                take("T", c)
                for hh in range(nh):
                    i = pe.matmul(psT[:, hh, :], pick[:, hh, :], f2row[:, :], start=True, stop=True)
                i.then_inc(f2_spread[q], 1)
                off = (1, 0, -1)[q]
                lend("T", c, max_made[q], lambda r: nh * NC * (r + off + 1))

            def rows(c):
                q = c.info
                pe.wait_ge(row_math[q], 8 * (c.b + 1))
                take("T", c)
                for n in range(NC):
                    i = pe.transpose(psT[0:8, 0, n * P:(n + 1) * P], c2[q][:, n, :, :].rearrange("p a h -> p (a h)"), ident[:, :])
                i.then_inc(c2_turned[q], 1)
                off = (1, 0, -1)[q]
                lend("T", c, rrow_made[q], lambda r: r + off + 1)

            def spread_(c):
                q, hh = (2, 0) if c.h == BACK else (c.h // 2, c.h % 2)
                pe.wait_ge(rrow_made[q], c.b + 1)
                wait(pe, arg_max, NC * c.unit)
                for w in range(2):
                    pe.matmul(psR[:, w, :], pick[:, 2 * w + hh, :], rrow[q][:, :], start=True, stop=True).then_inc(spread, 1)

            def attend(c):
                pe.wait_ge(prob_lo, c.unit + 1)
                if c.h == BACK:
                    pe.wait_ge(m2_read, 2 * (c.b + 1))
                    hi, low = (lambda j: w2x[:, j, :]), (lambda j: w2l[:, j, :])
                else:
                    pe.wait_ge(m1_read, 2 * H * c.b + 2 * c.h + 2)
                    hi, low = (lambda j: whx[:, j, c.h, :]), (lambda j: whl[:, j, c.h, :])
                take(c.pair, c)
                for n in range(2):
                    r = product(psA[c.pair][:, n, 0:F],
                                [(prob[0][:, c.buf, j, n * P:(n + 1) * P], prob[1][:, c.buf, j, n * P:(n + 1) * P], hi(j), low(j))
                                 for j in range(NC)], wide=psA[c.pair][:, n, 0:FA])
                r.then_inc(att_done, 1)
                lend(c.pair, c, elu_x, lambda r: unit_number(r, c.info) + 1)

            def turn2(c):
                pe.wait_ge(elu_out, c.before)
                take("T", c)
                for k in range(OC):
                    i = pe.transpose(psT[:, k // 4, (k % 4) * P:(k % 4 + 1) * P], hcat[:, c.info, k // KC, (k % KC) * P:(k % KC + 1) * P],
                                     ident[:, :])
                i.then_inc(m2_turned, 1)
                n = c.info
                lend("T", c, hx_lo, lambda r: NC * (r - 1) + n + 1)

            def mix2(c):
                pe.wait_ge(hx_lo, NC * c.b + c.info + 1)
                if c.info % 2 == 0:
                    take(c.pair, c)
                product(psA[c.pair][:, c.info % 2, 0:FA],
                        [(hx[0][:, k, :], hx[1][:, k, :], wo[0][:, k, :], wo[1][:, k, :]) for k in range(OC)]).then_inc(m2_done, 1)
                n = c.info
                lend(c.pair, c, m2_read, lambda r: 2 * (r - 1) + n // 2 + 1)

            def turn_out(c):
                pe.wait_ge(elu_out, unit_number(c.r, 5) + 1)
                take("T", c)
                for k in range(KC):
                    for n in range(NC):
                        i = pe.transpose(psT[:, k, n * P:(n + 1) * P], wk[:, n, k * P:(k + 1) * P], ident[:, :])
                i.then_inc(o_turned, 1)
                lend("T", c, oT_ready, lambda r: r)

            outT = ff[:, 0, :, :].rearrange("p c f -> p (c f)").rearrange("p (k n) -> p k n", k=KC)
            midT = ff[:, 1, :, :].rearrange("p c f -> p (c f)").rearrange("p (k n) -> p k n", k=KC)

            def ffn1(c):
                pe.wait_ge(oT_ready, c.b + 1)
                take(c.pair, c)
                for o in range(KC):
                    for k in range(KC):
                        i = pe.matmul(psA[c.pair][:, o, :], w1_sb[:, k, o * P:(o + 1) * P], outT[:, k, :], start=(k == 0), stop=(k == KC - 1))
                    i.then_inc(f1_done, 1)
                lend(c.pair, c, f1_read, lambda r: KC * r)

            def ffn2(c):
                pe.wait_ge(f1_read, KC * (c.b + 1))
                take(c.pair, c)
                for n in range(NC):
                    y = psA[c.pair][:, n // 2, (n % 2) * F:(n % 2 + 1) * F]
                    pe.matmul(y, pick[:, 1, :], brow[:, :], start=True, stop=False)
                    for k in range(KC):
                        i = pe.matmul(y, midT[:, k, n * P:(n + 1) * P], w2_sb[:, k, :], start=False, stop=(k == KC - 1))
                i.then_inc(f2_done, 1)
                lend(c.pair, c, y_ready, lambda r: r)

            def turn_gc(c):
                pe.wait_ge(ln_out["gc"], c.b + 1)
                take("T", c)
                for k in range(KC):
                    for n in range(NC):
                        i = pe.transpose(psT[:, k, n * P:(n + 1) * P], ff[:, 1, n, k * P:(k + 1) * P], ident[:, :])
                i.then_inc(h2_turned, 1)
                lend("T", c, h2_lo, lambda r: r)

            def conv_in_(c):
                pe.wait_ge(h2_lo, c.b + 1)
                take(c.pair, c)
                for i in range(2):
                    n = 2 * c.info + i
                    r = product(psA[c.pair][:, i, :],
                                [(h2T[0][:, k, n * P:(n + 1) * P], h2T[1][:, k, n * P:(n + 1) * P], wg[0][:, k, :], wg[1][:, k, :]) for k in range(KC)],
                                also=(psA[c.pair][:, i, 0:F], pick[:, 0, :], brow[:, :]))
                r.then_inc(conv_in, 1)
                p = c.info
                lend(c.pair, c, conv_in_read, lambda r: 2 * (r - 1) + p + 1)

            def conv(c):
                pe.wait_ge(mj_lo, 2 * (c.b + 1))
                take("T", c)
                for n in range(NC):
                    for j in range(NC):
                        for s, mj in enumerate((w2x[:, j, 0:F], w2l[:, j, :])):
                            i = pe.matmul(psT[:, n // 2, (n % 2) * F:(n % 2 + 1) * F], adjT[:, j, n * P:(n + 1) * P], mj,
                                          start=(j == 0 and s == 0), stop=(j == NC - 1 and s == 1))
                i.then_inc(conv_done, 1)
                lend("T", c, res_ready, lambda r: r)

            run_all(pe, PE_STEPS, {"turn_in": turn_in, "m1": m1, "f2rows": f2rows, "rowmax": rowmax, "rows": rows, "spread": spread_,
                         "attend": attend, "turn2": turn2, "mix2": mix2, "turn_out": turn_out, "ffn1": ffn1, "ffn2": ffn2,
                         "turn_gc": turn_gc, "conv_in": conv_in_, "conv": conv}, at_trip_end)


_INS = ["x", "adj", "L0_gnn_W_heads", "L0_gnn_a_heads", "L0_gnn_W_out", "L0_gnn_a_out", "L0_gnn_w1", "L0_gnn_b1",
        "L0_gnn_w2", "L0_gnn_b2", "L0_gnn_ln_gamma", "L0_gnn_ln_beta", "L1_gnn_W", "L1_gnn_b"]


def kernel(**inputs):
    import numpy as _np
    import concourse.bacc as _bacc
    from concourse import mybir as _mybir
    from concourse.bass_utils import run_bass_kernel_spmd as _run

    nc = _bacc.Bacc("TRN2", target_bir_lowering=False, num_devices=1)
    arrays, args = {}, []
    for name in _INS:
        a = _np.ascontiguousarray(inputs[name])
        arrays[f"in_{name}"] = a
        args.append(nc.dram_tensor(f"in_{name}", a.shape, _mybir.dt.from_np(a.dtype), kind="ExternalInput").ap())
    shape = arrays["in_x"].shape
    out = nc.dram_tensor("out_x", shape, _mybir.dt.float32, kind="ExternalOutput").ap()
    gnn_kernel(nc, *args, out)
    r = _run(nc, [arrays], core_ids=[0])
    return r.results[0]["out_x"]
```

```python
from contextlib import ExitStack

import concourse.bass as bass
from concourse import mybir



SP_STEPS = [
    ("load", 0, 0), ("conv", 0, 2), ("load_back", 0, 1),
]
PE_STEPS = [
    ("turn2", 2, 2), ("attend", 2, 2), ("turn2", 3, 2), ("mix2", 2, 2), ("mix2", 3, 2), ("m1", (0, 0), 2), ("f2rows", 2, 2),
    ("m1", (0, 1), 2), ("rowmax", (2, 0), 2), ("attend", 3, 2), ("f2rows", 1, 2), ("rowmax", (1, 0), 2), ("rows", 2, 2),
    ("rowmax", (1, 1), 2), ("spread", 4, 2), ("m1", (1, 0), 2), ("m1", (1, 1), 2), ("rows", 1, 2), ("spread", 6, 2),
    ("f2rows", 0, 2), ("attend", 4, 2), ("rowmax", (0, 0), 2), ("attend", 5, 2), ("rowmax", (0, 1), 2), ("spread", 8, 2),
    ("attend", 6, 2), ("turn_out", 0, 2), ("attend", 7, 2), ("ffn1", 0, 2), ("m1", (2, 0), 1), ("rows", 0, 2), ("ffn2", 0, 2),
    ("spread", 0, 1), ("m1", (2, 1), 1), ("attend", 8, 2), ("turn_in", 0, 1), ("attend", 9, 2), ("m1", (3, 0), 1),
    ("m1", (3, 1), 1), ("spread", 2, 1), ("attend", 0, 1), ("turn_gc", 0, 2), ("attend", 1, 1), ("conv_in", 0, 2),
    ("turn2", 0, 1), ("conv_in", 1, 2), ("turn2", 1, 1), ("mix2", 0, 1), ("conv", 0, 2), ("mix2", 1, 1),
]
ACT_STEPS = [
    ("mix2", 0, 2), ("turn2", 2, 2), ("elu_out", 1, 2), ("probs", 3, 2), ("turn2", 3, 2), ("elu_in", 2, 2), ("elu_out", 2, 2),
    ("mix2", 1, 2), ("m1", (0, 0), 2), ("f2rows", 2, 2), ("m1", (0, 1), 2), ("norm_in_out", 0, 1), ("elu_in", 3, 2),
    ("f2rows", 1, 2), ("rows", 2, 2), ("elu_out", 3, 2), ("args", 4, 2), ("args", 5, 2), ("probs", 4, 2), ("m1", (1, 0), 2),
    ("probs", 5, 2), ("m1", (1, 1), 2), ("rows", 1, 2), ("args", 6, 2), ("args", 7, 2), ("f2rows", 0, 2), ("elu_in", 4, 2),
    ("probs", 6, 2), ("elu_out", 4, 2), ("elu_in", 5, 2), ("probs", 7, 2), ("elu_out", 5, 2), ("args", 8, 2),
    ("turn_out", 0, 2), ("elu_in", 6, 2), ("args", 9, 2), ("elu_out", 6, 2), ("elu_in", 7, 2), ("ffn1", 0, 2), ("probs", 8, 2),
    ("m1", (2, 0), 1), ("rows", 0, 2), ("probs", 9, 2), ("args", 0, 1), ("m1", (2, 1), 1), ("elu_out", 7, 2), ("args", 1, 1),
    ("norm_ff_out", 0, 2), ("elu_in", 8, 2), ("probs", 0, 1), ("elu_out", 8, 2), ("elu_in", 9, 2), ("m1", (3, 0), 1),
    ("probs", 1, 1), ("m1", (3, 1), 1), ("turn_in", 0, 1), ("norm_gc_out", 0, 2), ("args", 2, 1), ("turn_gc", 0, 2),
    ("elu_in", 0, 1), ("elu_out", 9, 2), ("args", 3, 1), ("elu_in", 1, 1), ("conv_in", 0, 2), ("turn2", 0, 1), ("probs", 2, 1),
    ("conv_in", 1, 2), ("turn2", 1, 1), ("elu_out", 0, 1),
]
DVE_STEPS = [
    ("elu_neg", 1, 2), ("turn2", 2, 2), ("mix2", 0, 2), ("elu_in", 2, 2), ("turn2", 3, 2), ("elu_out", 1, 2), ("elu_neg", 2, 2),
    ("mix2", 1, 2), ("f2rows", 2, 2), ("m1", (0, 0), 2), ("elu_out", 2, 2), ("norm_in_out", 0, 1), ("rowmax", (2, 0), 2),
    ("elu_in", 3, 2), ("rowmath", 2, 2), ("elu_neg", 3, 2), ("rowmax", (1, 0), 2), ("args", 4, 2), ("m1", (0, 1), 2),
    ("args", 5, 2), ("rowmax", (1, 1), 2), ("rowmath", 1, 2), ("m1", (1, 0), 2), ("elu_out", 3, 2), ("m1", (1, 1), 2),
    ("f2rows", 0, 2), ("args", 6, 2), ("args", 7, 2), ("elu_in", 4, 2), ("rowmax", (0, 0), 2), ("elu_neg", 4, 2),
    ("elu_in", 5, 2), ("rowmax", (0, 1), 2), ("elu_out", 4, 2), ("elu_neg", 5, 2), ("elu_out", 5, 2), ("args", 8, 2),
    ("elu_in", 6, 2), ("rowmath", 0, 2), ("elu_neg", 6, 2), ("elu_in", 7, 2), ("args", 9, 2), ("elu_out", 6, 2),
    ("m1", (2, 0), 1), ("elu_neg", 7, 2), ("ffn2", 0, 2), ("norm_ff", 0, 2), ("args", 0, 1), ("norm_ff_out", 0, 2),
    ("m1", (2, 1), 1), ("elu_in", 8, 2), ("args", 1, 1), ("elu_out", 7, 2), ("elu_neg", 8, 2), ("elu_in", 9, 2), ("x2", 0, 2),
    ("norm_gc", 0, 2), ("elu_out", 8, 2), ("m1", (3, 0), 1), ("m1", (3, 1), 1), ("norm_gc_out", 0, 2), ("elu_neg", 9, 2),
    ("turn_in", 0, 1), ("elu_in", 0, 1), ("args", 2, 1), ("turn_gc", 0, 2), ("elu_out", 9, 2), ("elu_neg", 0, 1),
    ("elu_in", 1, 1), ("f2rows", 1, 1), ("conv_in", 0, 2), ("turn2", 0, 1), ("conv_in", 1, 2), ("turn2", 1, 1), ("args", 3, 1),
    ("norm_in", 0, 0), ("elu_out", 0, 1), ("conv", 0, 2),
]
POOL_STEPS = [
    ("probs", 3, 2), ("x_beta", 0, 2), ("norm_in", 0, 1), ("args", 4, 2), ("args", 5, 2), ("probs", 4, 2), ("probs", 5, 2),
    ("args", 6, 2), ("args", 7, 2), ("probs", 6, 2), ("probs", 7, 2), ("args", 8, 2), ("args", 9, 2), ("probs", 8, 2),
    ("probs", 9, 2), ("norm_ff", 0, 2), ("args", 0, 1), ("gamma", 0, 2), ("args", 1, 1), ("probs", 0, 1), ("norm_gc", 0, 2),
    ("probs", 1, 1), ("args", 2, 1), ("probs", 2, 1), ("args", 3, 1),
]


def gnn_kernel(nc, x, adj, W_heads, a_heads, W_out, a_out, w1, b1, w2, b2, gamma, beta, W_gc, b_gc, out):
    fp32, f32r, bf16, i32 = mybir.dt.float32, mybir.dt.float32r, mybir.dt.bfloat16, mybir.dt.int32
    ALU = mybir.AluOpType
    ACT = mybir.ActivationFunctionType
    AX = mybir.AxisListType

    P = 128
    B, N, F = x.shape
    H = W_heads.shape[0]
    NC = N // P
    KC = F // P
    OC = H * KC
    HN = N // 2
    FA = F + 2
    UN = 2 * H
    SLOPE = 0.01
    EPS = 1e-5
    BIG = 2.0 ** 100

    x_v = x.rearrange("b (c p) f -> b p c f", p=P)
    out_v = out.rearrange("b (c p) f -> b p c f", p=P)

    ctx = ExitStack()
    with ctx:
        def sb(name, shape, dt=fp32):
            return ctx.enter_context(nc.sbuf_tensor(name, shape, dt))

        def sem(name):
            return ctx.enter_context(nc.semaphore(name))

        wh = [sb(f"wh_{s}", [P, KC, H, FA], f32r) for s in ("hi", "lo")]
        wo = [sb(f"wo_{s}", [P, OC, FA], f32r) for s in ("hi", "lo")]
        w1_sb = sb("w1_sb", [P, KC, F])
        w2_sb = sb("w2_sb", [P, KC, F])
        wg = [sb(f"wg_{s}", [P, KC, 2 * F], f32r) for s in ("hi", "lo")]
        adjT = sb("adjT", [P, NC, N], f32r)
        maskT = sb("maskT", [P, NC, N], bf16)
        mask = sb("mask", [P, NC, N], bf16)
        deg = sb("deg", [P, NC])
        brow = sb("brow", [P, F], f32r)
        ident = sb("ident", [P, P])
        b1c = sb("b1c", [P, KC])
        gamma_bc = sb("gamma_bc", [P, F])
        beta_bc = sb("beta_bc", [P, F])
        pick = sb("pick", [P, 4, P], f32r)
        mhalf = sb("mhalf", [P, NC])

        xin = sb("xin", [P, NC, F])
        hT = [sb(f"hT_{s}", [P, KC, N], f32r) for s in ("hi", "lo")]
        whx = sb("whx_hi", [P, NC, H, FA], f32r)
        whl = sb("whx_lo", [P, NC, H, F], f32r)
        w2x = sb("w2x_hi", [P, NC, FA], f32r)
        w2l = sb("w2x_lo", [P, NC, F], f32r)
        arg = sb("arg", [P, 2, NC, HN])
        prob = [sb(f"prob_{s}", [P, 2, NC, HN], f32r) for s in ("hi", "lo")]
        elu_in = sb("elu_in", [P, 2, 2, F])
        elu_ex = sb("elu_ex", [P, 2, F])
        hcat = sb("hcat", [P, NC, H, F])
        hx = [sb(f"hx_{s}", [P, 8, P], f32r) for s in ("hi", "lo")]
        ff = sb("ff", [P, 2, NC, F])
        h2T = [sb(f"h2T_{s}", [P, KC, N], f32r) for s in ("hi", "lo")]
        turned = (hx, [h[:, :, :].rearrange("p a n -> p (a n)").rearrange("p (k n) -> p k n", k=OC) for h in h2T])
        wk = sb("wk", [P, NC, F])
        xb = sb("xb", [P, NC, F])
        junk = sb("junk", [P, 2, N], bf16)
        held = sb("held", [P, 3])
        fcol = sb("fcol", [P, NC, H, 2])
        fcol2 = sb("fcol2", [P, NC, 1, 2])
        fs = sb("fs", [P, NC, H])
        fs2 = sb("fs2", [P, NC, 1])
        c1 = [sb(f"c1_{q}", [P, NC, 2, 2]) for q in range(3)]
        c2 = [sb(f"c2_{q}", [P, NC, 4, 2]) for q in range(3)]
        gmax = [sb(f"gmax_{q}", [P, NC, 2]) for q in range(3)]
        zrow = [sb(f"zrow_{q}", [P, 4, NC, 2]) for q in range(3)]
        f2row = sb("f2row", [P, N], f32r)
        rrow = [sb(f"rrow_{q}", [P, N], f32r) for q in range(3)]
        rec = sb("rec", [P, 2, 2])
        st = sb("st", [P, NC, 6])
        NORMS = ("in", "ff", "gc")
        mv = {k: sb(f"mv_{k}", [P, NC, 2]) for k in NORMS}
        ve = {k: sb(f"ve_{k}", [P, NC]) for k in NORMS}
        rstd = {k: sb(f"rstd_{k}", [P, NC]) for k in NORMS}
        shift = {k: sb(f"shift_{k}", [P, NC]) for k in NORMS}

        pick_st = elu_in[:, :, :, :].rearrange("p a c f -> p (a c f)").rearrange("p (w h m) -> p w h m", w=2, h=2, m=2 * P)[:, :, :, 0:P]
        identb = elu_ex[:, 1, 0:P // 2].bitcast(bf16)
        cnt, lone = elu_ex[:, 0, 0:NC], elu_ex[:, 0, NC:2 * NC]
        wsum = elu_ex[:, 0, 0:2 * OC].rearrange("p (k h s) -> p k h s", k=KC, h=H)
        wsum2 = elu_ex[:, 0, 2 * OC:4 * OC].rearrange("p (k s) -> p k s", k=OC)
        psA = [ctx.enter_context(nc.psum_tensor(f"psA{i}", [P, 2, 512], fp32)) for i in range(2)]
        psT = ctx.enter_context(nc.psum_tensor("psT", [P, 2, 512], fp32))
        psR = ctx.enter_context(nc.psum_tensor("psR", [P, 2, 512], fp32))

        NLOAD = 13
        ld = [sem(f"ld{i}") for i in range(NLOAD)]
        LD_ADJ, LD_WH, LD_A, LD_WO, LD_AO, LD_GC, LD_W1, LD_W2, LD_B1, LD_B2, LD_G, LD_BE, LD_BG = range(NLOAD)
        s_zeroed = sem("s_zeroed")
        s_const = sem("s_const")
        s_adj = sem("s_adj")
        s_adj_turned = sem("s_adj_turned")
        s_adj_out = sem("s_adj_out")
        s_gc_turned = sem("s_gc_turned")
        s_gc_hi = sem("s_gc_hi")
        s_cleared = sem("s_cleared")
        s_setup = sem("s_setup")
        s_setup_back = sem("s_setup_back")
        s_hi = sem("s_hi")
        s_dve = sem("s_dve")

        x_loaded = sem("x_loaded")
        ln_stat = {k: sem(f"ln_stat_{k}") for k in NORMS}
        ln_aggr = {k: sem(f"ln_aggr_{k}") for k in NORMS}
        ln_var = {k: sem(f"ln_var_{k}") for k in NORMS}
        ln_rstd = {k: sem(f"ln_rstd_{k}") for k in NORMS}
        ln_shift = {k: sem(f"ln_shift_{k}") for k in NORMS}
        ln_out = {k: sem(f"ln_out_{k}") for k in NORMS}
        h_turned = sem("h_turned")
        hT_hi = sem("hT_hi_ready")
        hT_lo = sem("hT_lo_ready")
        m1_done = sem("m1_done")
        m1_hi = sem("m1_hi")
        m1_lo = sem("m1_lo")
        m1_read = sem("m1_read")
        c1_made = [sem(f"c1_made{q}") for q in range(3)]
        c1_turned = [sem(f"c1_turned{q}") for q in range(3)]
        f2row_made = [sem(f"f2row_made{q}") for q in range(3)]
        f2_spread = [sem(f"f2_spread{q}") for q in range(3)]
        max_made = [sem(f"max_made{q}") for q in range(3)]
        row_math = [sem(f"row_math{q}") for q in range(3)]
        c2_turned = [sem(f"c2_turned{q}") for q in range(3)]
        rrow_made = [sem(f"rrow_made{q}") for q in range(3)]
        m2_turned = sem("m2_turned")
        hx_hi = sem("hx_hi_ready")
        hx_lo = sem("hx_lo_ready")
        m2_done = sem("m2_done")
        m2_hi = sem("m2_hi")
        m2_lo = sem("m2_lo")
        m2_read = sem("m2_read")
        xb_loaded = sem("xb_loaded")
        o_turned = sem("o_turned")
        oT_ready = sem("oT_ready")
        x_beta = sem("x_beta")
        f1_done = sem("f1_done")
        f1_read = sem("f1_read")
        f2_done = sem("f2_done")
        y_ready = sem("y_ready")
        y_gamma = sem("y_gamma")
        x2_ready = sem("x2_ready")
        h2_turned = sem("h2_turned")
        h2_hi = sem("h2_hi")
        h2_lo = sem("h2_lo")
        conv_in = sem("conv_in")
        mj_hi = sem("mj_hi")
        mj_lo = sem("mj_lo")
        conv_in_read = sem("conv_in_read")
        conv_done = sem("conv_done")
        res_ready = sem("res_ready")
        stored = sem("stored")

        spread = sem("spread")
        arg_lin = sem("arg_lin")
        arg_max = sem("arg_max")
        arg_masked = sem("arg_masked")
        prob_hi = sem("prob_hi")
        prob_exp = sem("prob_exp")
        prob_lo = sem("prob_lo")
        att_done = sem("att_done")
        elu_rec = sem("elu_rec")
        elu_x = sem("elu_x")
        elu_neg = sem("elu_neg")
        elu_exp = sem("elu_exp")
        elu_out = sem("elu_out")

        block = ctx.enter_context(nc.Block())

        def wait(eng, s, count):
            if not isinstance(count, int) or count > 0:
                eng.wait_ge(s, count)

        BACK = -1
        UNITS = [(0, 0), (0, 1), (1, 0), (1, 1), (BACK, 0), (BACK, 1), (2, 0), (2, 1), (3, 0), (3, 1)]
        UNIT_STEPS = ("spread", "args", "probs", "attend", "elu_in", "elu_neg", "elu_out")
        IN_PSA = ("m1", "attend", "mix2", "ffn1", "ffn2", "conv_in")

        def batch_of(name, info, r):
            if name in UNIT_STEPS:
                return r - 1 if UNITS[info][0] == BACK else r
            if name == "m1":
                return r if info[0] >= 2 else r + 1
            if name in ("f2rows", "rowmax", "rowmath", "rows"):
                return (r + 1, r, r - 1)[info[0] if name == "rowmax" else info]
            return r + 1 if name in ("load", "norm_in", "norm_in_out", "turn_in") else r - 1

        def units_before(r):
            return 0 if isinstance(r, int) and r <= 0 else (UN + 2) * r - 2

        def unit_number(r, s):
            if isinstance(r, int) and (r == 0 and s >= 4 or r == B):
                s = s - 2 if r == 0 else s - 4
            return units_before(r) + s

        def psa_pairs():
            users = []
            for name, info, _ in PE_STEPS:
                key = (name, info // 2 if name == "mix2" else info)
                if name in IN_PSA and key not in users:
                    users.append(key)
            assert len(users) % 2 == 0
            return {key: k % 2 for k, key in enumerate(users)}

        pair_of = psa_pairs()
        LATEST = max(late for table in (SP_STEPS, PE_STEPS, ACT_STEPS, DVE_STEPS, POOL_STEPS) for _, _, late in table)

        class Step:
            pass

        def run_all(eng, table, steps_of, at_trip_end=lambda: None, after_first=lambda: None):
            def trip(t):
                for name, info, late in table:
                    c = Step()
                    c.r, c.late, c.info = t - late, late, info
                    c.b = batch_of(name, info, c.r)
                    if isinstance(c.b, int) and not 0 <= c.b < B:
                        continue
                    c.before = units_before(c.r)
                    if name in UNIT_STEPS:
                        c.h, c.u = UNITS[info]
                        c.unit, c.buf = unit_number(c.r, info), info % 2
                    c.pair = pair_of.get(("attend" if name == "elu_in" else name,
                                          info // 2 if name == "mix2" and table is PE_STEPS else info))
                    steps_of[name](c)
                at_trip_end()

            for t in range(-1, 2 + LATEST):
                trip(t)
                if t == -1:
                    after_first()
            with eng.Fori(2 + LATEST, B - 1) as t:
                trip(t)
            for t in range(B - 1, B + 1 + LATEST):
                trip(t)

        def heads_of(q):
            return (0, 2) if q == 0 else (2, 2) if q == 1 else (0, 1)

        @block.sync
        def _(sp):
            sp.dma_start(arg[:, :, :, :].rearrange("p a c n -> p (a c n)").bitcast(i32).rearrange("p (c n) -> p c n", c=NC),
                         adj.rearrange("(c p) n -> p c n", p=P)).then_inc(ld[LD_ADJ], 16)
            sp.dma_start(xb[:, :, :].rearrange("p (a c) f -> p a (c f)", a=2), W_gc.rearrange("(a p) d -> p a d", p=P)).then_inc(ld[LD_GC], 16)
            for k in range(KC):
                sp.dma_start(hcat[:, k, :, :], W_heads[:, k * P:(k + 1) * P, :].rearrange("h p o -> p h o")).then_inc(ld[LD_WH], 16)
            sp.dma_start(ff[:, :, :, :].rearrange("p a c f -> p (a c f)").rearrange("p (h f) -> p h f", h=H),
                         a_heads.partition_broadcast(P)).then_inc(ld[LD_A], 16)
            sp.dma_start(hcat[:, KC:NC, :, :].rearrange("p a h f -> p (a h) f"), W_out.rearrange("(k p) o -> p k o", p=P)).then_inc(ld[LD_WO], 16)
            sp.dma_start(wk[:, 0:2, :].rearrange("p c f -> p (c f)"), a_out.partition_broadcast(P)).then_inc(ld[LD_AO], 16)
            sp.dma_start(wk[:, 2, :], b_gc.partition_broadcast(P)).then_inc(ld[LD_BG], 16)
            sp.dma_start(w1_sb[:, :, :], w1.rearrange("(k p) o -> p k o", p=P)).then_inc(ld[LD_W1], 16)
            sp.dma_start(w2_sb[:, :, :], w2.rearrange("(k p) o -> p k o", p=P)).then_inc(ld[LD_W2], 16)
            sp.dma_start(b1c[:, :], b1.rearrange("(k p) -> p k", p=P), allow_slow_non_contiguous=True).then_inc(ld[LD_B1], 16)
            sp.dma_start(wk[:, 3, :], b2.partition_broadcast(P)).then_inc(ld[LD_B2], 16)
            sp.dma_start(gamma_bc[:, :], gamma.partition_broadcast(P)).then_inc(ld[LD_G], 16)
            sp.dma_start(beta_bc[:, :], beta.partition_broadcast(P)).then_inc(ld[LD_BE], 16)

            def load(c):
                wait(sp, h_turned, c.b)
                sp.dma_start(xin[:, :, :], x_v[c.b]).then_inc(x_loaded, 16)

            def load_back(c):
                wait(sp, s_setup, 1)
                wait(sp, stored, 16 * c.b)
                sp.dma_start(xb[:, :, :], x_v[c.b]).then_inc(xb_loaded, 16)

            def conv(c):
                wait(sp, res_ready, c.b + 1)
                sp.dma_start(out_v[c.b], xb[:, :, :]).then_inc(stored, 16)

            run_all(sp, SP_STEPS, {"load": load, "load_back": load_back, "conv": conv})
            sp.wait_ge(stored, 16 * B)

        @block.gpsimd
        def _(pool):
            pool.memset(ident[:, :], 0.0).then_inc(s_zeroed, 1)
            pool.memset(mhalf[:, :], -0.5).then_inc(s_zeroed, 1)
            pool.memset(pick_st, 0.0).then_inc(s_zeroed, 1)
            pool.wait_ge(s_zeroed, 3)
            pool.affine_select(out=ident[:, :], in_=ident[:, :], compare_op=ALU.not_equal, fill=1.0, base=0,
                               pattern=[[-1, P]], channel_multiplier=1).then_inc(s_const, 1)
            for z in range(2):
                pool.affine_select(out=pick_st, in_=pick_st, compare_op=ALU.not_equal, fill=1.0, base=-2 * z,
                                   pattern=[[-4, 2], [-1, 2], [0, P]], channel_multiplier=1).then_inc(s_const, 1)
                pool.wait_ge(s_const, 2 + z)
            pool.memset(f2row[:, :].bitcast(fp32), 0.0)
            for q in range(3):
                pool.memset(rrow[q][:, :].bitcast(fp32), 0.0)
                pool.memset(c1[q][:, :, :, :], 0.0)
                i = pool.memset(c2[q][:, :, :, :], 0.0)
            i.then_inc(s_cleared, 1)

            def norm(k):
                def step(c):
                    pool.wait_ge(ln_var[k], c.b + 1)
                    pool.tensor_tensor(out=rstd[k][:, :], in0=ve[k][:, :], in1=mhalf[:, :], op=ALU.pow).then_inc(ln_rstd[k], 1)
                return step

            def args(c):
                pool.wait_ge(arg_max, NC * (c.unit + 1))
                a = arg[:, c.buf, :, :]
                pool.tensor_tensor(out=a, in0=a, in1=maskT[:, :, c.u * HN:(c.u + 1) * HN], op=ALU.add).then_inc(arg_masked, 1)

            def probs(c):
                pool.wait_ge(prob_exp, c.unit + 1)
                pool.tensor_tensor(out=prob[1][:, c.buf, :, :], in0=arg[:, c.buf, :, :], in1=prob[0][:, c.buf, :, :].bitcast(fp32),
                                   op=ALU.subtract).then_inc(prob_lo, 1)

            def x_beta_(c):
                pool.wait_ge(xb_loaded, 16 * (c.b + 1))
                pool.tensor_tensor(out=xb[:, :, :], in0=xb[:, :, :], in1=beta_bc[:, None, :].to_broadcast([P, NC, F]),
                                   op=ALU.add).then_inc(x_beta, 1)

            def gamma_(c):
                pool.wait_ge(ln_out["ff"], c.b + 1)
                pool.tensor_tensor(out=wk[:, :, :], in0=wk[:, :, :], in1=gamma_bc[:, None, :].to_broadcast([P, NC, F]),
                                   op=ALU.mult).then_inc(y_gamma, 1)

            for l in (LD_G, LD_BE):
                pool.wait_ge(ld[l], 16)
            pool.wait_ge(s_setup, 1)
            run_all(pool, POOL_STEPS, {"norm_in": norm("in"), "args": args, "probs": probs, "x_beta": x_beta_,
                                       "norm_ff": norm("ff"), "gamma": gamma_, "norm_gc": norm("gc")})

        @block.scalar
        def _(act):
            act.wait_ge(ld[LD_WH], 16 * KC)
            act.activation(wh[0][:, :, :, 0:F], hcat[:, 0:KC, :, :], ACT.Copy).then_inc(s_hi, 1)
            act.wait_ge(ld[LD_WO], 16)
            act.activation(wo[0][:, :, 0:F], hcat[:, KC:NC, :, :].rearrange("p a h f -> p (a h) f"), ACT.Copy).then_inc(s_hi, 1)
            act.wait_ge(s_gc_turned, 1)
            act.activation(wg[0][:, :, :], psR[:, :, :], ACT.Copy).then_inc(s_gc_hi, 1)
            act.wait_ge(ld[LD_B1], 16)
            act.wait_ge(s_setup, 1)

            def norm_out(k, src, dst, func):
                def step(c):
                    act.wait_ge(ln_shift[k], c.b + 1)
                    for n in range(NC):
                        i = act.activation(dst[:, n, :], src[:, n, :], func, bias=shift[k][:, n:n + 1],
                                           scale=rstd[k][:, n:n + 1])
                    i.then_inc(ln_out[k], 1)
                return step

            def turn_in(c):
                act.wait_ge(h_turned, c.b + 1)
                wait(act, m1_done, 2 * H * c.b)
                act.activation(hT[0][:, :, :], psT[:, :, :], ACT.Copy).then_inc(hT_hi, 1)

            def m1(c):
                h, p = c.info
                act.wait_ge(m1_done, 2 * H * c.b + 2 * h + p + 1)
                if not isinstance(c.b, int) or c.b > 0:
                    wait(act, att_done, c.before + (2 * h + 2 if h < 2 else -2 if h == 2 else 0))
                act.activation(whx[:, 2 * p:2 * p + 2, h, 0:F], psA[c.pair][:, :, 0:F], ACT.Copy).then_inc(m1_hi, 1)

            def f2rows(c):
                q = c.info
                act.wait_ge(c1_turned[q], c.b + 1)
                act.activation(f2row[0:4, :], psT[0:4, 0, :], ACT.Copy).then_inc(f2row_made[q], 1)

            def rows(c):
                q = c.info
                act.wait_ge(c2_turned[q], c.b + 1)
                if not isinstance(c.b, int) or c.b > 0:
                    wait(act, spread, c.before + (4, 0, -4)[q])
                act.activation(rrow[q][0:8, :], psT[0:8, 1, :], ACT.Copy).then_inc(rrow_made[q], 1)

            def args(c):
                act.wait_ge(spread, c.unit - c.u + 2)
                wait(act, prob_lo, c.unit - 1)
                f = fs2[:, :, 0] if c.h == BACK else fs[:, :, c.h]
                for j in range(NC):
                    act.activation(arg[:, c.buf, j, :], psR[:, 1, c.u * HN:(c.u + 1) * HN], ACT.Identity,
                                   bias=f[:, j:j + 1]).then_inc(arg_lin, 1)

            def probs(c):
                act.wait_ge(arg_masked, c.unit + 1)
                wait(act, att_done, c.unit - 1)
                act.activation(prob[0][:, c.buf, :, :], arg[:, c.buf, :, :], ACT.Exp).then_inc(prob_hi, 1)
                act.activation(arg[:, c.buf, :, :], arg[:, c.buf, :, :], ACT.Exp).then_inc(prob_exp, 1)

            def elu_in_(c):
                act.wait_ge(elu_rec, c.unit + 1)
                wait(act, elu_out, c.unit - 1)
                for n in range(2):
                    i = act.activation(elu_in[:, c.buf, n, :], psA[c.pair][:, n, 0:F], ACT.Copy,
                                       scale=rec[:, c.buf, n:n + 1])
                i.then_inc(elu_x, 1)

            def elu_out_(c):
                act.wait_ge(elu_neg, c.unit + 1)
                act.activation(elu_ex[:, :, :], elu_ex[:, :, :], ACT.Exp).then_inc(elu_exp, 1)

            def turn2(c):
                act.wait_ge(m2_turned, NC * c.b + c.info + 1)
                if c.info == 1:
                    wait(act, conv_in, 2 * c.b)
                else:
                    wait(act, m2_done, NC * c.b + c.info - 1)
                act.activation(turned[c.info % 2][0][:, :, :], psT[:, :, :].rearrange("p a n -> p (a n)").rearrange("p (k n) -> p k n", k=OC),
                               ACT.Copy).then_inc(hx_hi, 1)

            def mix2(c):
                act.wait_ge(m2_done, NC * c.b + 2 * c.info + 2)
                wait(act, conv_done, c.b)
                act.activation(w2x[:, 2 * c.info:2 * c.info + 2, 0:F], psA[c.pair][:, :, 0:F], ACT.Copy).then_inc(m2_hi, 1)

            def turn_out(c):
                act.wait_ge(o_turned, c.b + 1)
                act.activation(ff[:, 0, :, :], psT[:, :, :].rearrange("p a n -> p (a n)").rearrange("p (k n) -> p k n", k=NC),
                               ACT.Copy).then_inc(oT_ready, 1)

            def ffn1(c):
                for o in range(KC):
                    act.wait_ge(f1_done, KC * c.b + o + 1)
                    act.activation(ff[:, 1, 2 * o:2 * o + 2, :].rearrange("p c f -> p (c f)"), psA[c.pair][:, o, :], ACT.Relu,
                                   bias=b1c[:, o:o + 1]).then_inc(f1_read, 1)

            def turn_gc(c):
                act.wait_ge(h2_turned, c.b + 1)
                act.wait_ge(m2_done, NC * (c.b + 1))
                act.activation(h2T[0][:, :, :], psT[:, :, :], ACT.Copy).then_inc(h2_hi, 1)

            def conv_in_(c):
                act.wait_ge(conv_in, 2 * c.b + c.info + 1)
                act.activation(w2x[:, 2 * c.info:2 * c.info + 2, 0:F], psA[c.pair][:, :, F:2 * F], ACT.Copy).then_inc(mj_hi, 1)

            run_all(act, ACT_STEPS, {"norm_in_out": norm_out("in", xin, xin, ACT.Relu), "turn_in": turn_in, "m1": m1, "f2rows": f2rows,
                          "rows": rows, "args": args, "probs": probs, "elu_in": elu_in_, "elu_out": elu_out_,
                          "turn2": turn2, "mix2": mix2, "turn_out": turn_out, "ffn1": ffn1,
                          "norm_ff_out": norm_out("ff", wk, wk, ACT.Identity),
                          "norm_gc_out": norm_out("gc", xb, ff[:, 1, :, :], ACT.Relu),
                          "turn_gc": turn_gc, "conv_in": conv_in_})

        @block.vector
        def _(dve):
            count = [0]

            def link(ins):
                count[0] += 1
                ins.then_inc(s_dve, 1)
                dve.wait_ge(s_dve, count[0])

            adj_f = arg[:, :, :, :].rearrange("p a c n -> p (a c n)").rearrange("p (c n) -> p c n", c=NC)
            dve.wait_ge(ld[LD_ADJ], 16)
            link(dve.tensor_copy(adj_f, adj_f.bitcast(i32)))
            dve.tensor_scalar(mask[:, :, :], adj_f, 0.0, 1.0, ALU.is_gt, ALU.mult).then_inc(s_adj, 1)
            dve.wait_ge(s_adj, 1)
            link(dve.tensor_reduce(out=cnt, in_=mask[:, :, :], axis=AX.X, op=ALU.add))
            link(dve.tensor_scalar(lone, cnt, 0.0, 2.0 * BIG, ALU.is_equal, ALU.mult))
            link(dve.tensor_scalar(lone, lone, -BIG, None, ALU.add))
            dve.wait_ge(s_const, 3)
            link(dve.tensor_copy(identb, ident[:, :]))
            for n in range(NC):
                dve.tensor_scalar(mask[:, n, :], mask[:, n, :], BIG, lone[:, n:n + 1], ALU.mult, ALU.add).then_inc(s_adj, 1)
            link(dve.tensor_copy(pick[:, :, :].rearrange("p (w h) m -> p w h m", w=2), pick_st))
            dve.memset(whx[:, :, :, F:FA].bitcast(fp32), 1.0)
            link(dve.memset(w2x[:, :, F:FA].bitcast(fp32), 1.0))
            for n in range(NC):
                dve.wait_ge(s_adj_turned, n + 1)
                dve.tensor_copy(adjT[:, :, n * P:(n + 1) * P], psT[:, n % 2, :].rearrange("p (j i) -> p j i", j=NC))
                dve.tensor_copy(maskT[:, :, n * P:(n + 1) * P],
                                psA[n % 2][:, 0, 0:N // 2].bitcast(bf16).rearrange("p (j i) -> p j i", j=NC)).then_inc(s_adj_out, 1)
            dve.wait_ge(s_gc_hi, 1)
            dve.tensor_tensor(out=wg[1][:, :, :], in0=psR[:, :, :], in1=wg[0][:, :, :].bitcast(fp32), op=ALU.subtract)
            a_h = ff[:, :, :, :].rearrange("p a c f -> p (a c f)").rearrange("p (h s f) -> p h s f", h=H, s=2)
            a_o = wk[:, 0:2, :]
            w_o = hcat[:, KC:NC, :, :].rearrange("p a h f -> p (a h) f")
            lots = junk[:, :, :].rearrange("p a (b f) -> p (a b) f", f=F)

            def dot(k, a, b_, out):
                i = dve.tensor_tensor_reduce(out=lots[:, k % 4, :], in0=a, in1=b_, scale=1.0, scalar=0.0, op0=ALU.mult,
                                             op1=ALU.add, accum_out=out)
                if k % 4 == 3:
                    link(i)

            dve.wait_ge(ld[LD_WH], 16 * KC)
            dve.wait_ge(ld[LD_A], 16)
            for k in range(2 * KC * H):
                h, kc, s = k % H, k // H % KC, k // (H * KC)
                dot(k, hcat[:, kc, h, :], a_h[:, h, s, :], wsum[:, kc, h, s:s + 1])
            link(dve.tensor_copy(wh[0][:, :, :, F:FA], wsum))
            dve.wait_ge(s_hi, 2)
            for k in range(KC):
                dve.tensor_tensor(out=wh[1][:, k, :, F:FA], in0=wsum[:, k, :, :], in1=wh[0][:, k, :, F:FA].bitcast(fp32), op=ALU.subtract)
                dve.tensor_tensor(out=wh[1][:, k, :, 0:F], in0=hcat[:, k, :, :], in1=wh[0][:, k, :, 0:F].bitcast(fp32), op=ALU.subtract)
            dve.wait_ge(s_cleared, 1)
            link(dve.memset(junk[:, 0, 0:2], 0.0))
            dve.memset(junk[:, 0, 2:4], 0.0).then_inc(s_setup, 1)

            def setup_back():
                link(dve.tensor_reduce(out=deg[:, :], in_=adj_f, axis=AX.X, op=ALU.add))
                for l in (LD_BG, LD_B2):
                    dve.wait_ge(ld[l], 16)
                for k in range(2):
                    link(dve.tensor_copy(w2x[:, k, 0:F], wk[:, 2 + k, :]))
                    link(dve.tensor_tensor(out=elu_ex[:, k, :], in0=wk[:, 2 + k, :], in1=w2x[:, k, 0:F].bitcast(fp32), op=ALU.subtract))
                    link(dve.tensor_scalar(elu_ex[:, k, :], elu_ex[:, k, :], ident[:, 2 + k:3 + k], None, ALU.mult))
                    link(dve.scalar_tensor_tensor(out=elu_ex[:, k, :], in0=w2x[:, k, 0:F].bitcast(fp32), scalar=ident[:, k:k + 1],
                                                  in1=elu_ex[:, k, :], op0=ALU.mult, op1=ALU.add))
                link(dve.tensor_tensor(out=brow[:, :], in0=elu_ex[:, 0, :], in1=elu_ex[:, 1, :], op=ALU.add))
                for l in (LD_WO, LD_AO):
                    dve.wait_ge(ld[l], 16)
                for k in range(2 * OC):
                    dot(k, w_o[:, k // 2, :], a_o[:, k % 2, :], wsum2[:, k // 2, k % 2:k % 2 + 1])
                link(dve.tensor_copy(wo[0][:, :, F:FA], wsum2))
                dve.tensor_tensor(out=wo[1][:, :, F:FA], in0=wsum2, in1=wo[0][:, :, F:FA].bitcast(fp32), op=ALU.subtract)
                dve.tensor_tensor(out=wo[1][:, :, 0:F], in0=w_o, in1=wo[0][:, :, 0:F].bitcast(fp32),
                                  op=ALU.subtract).then_inc(s_setup_back, 1)

            def norm(k, src, ready, per):
                def step(c):
                    dve.wait_ge(ready, per * (c.b + 1))
                    for n in range(NC):
                        i = dve.bn_stats(st[:, n, :], src[:, n, :])
                    i.then_inc(ln_stat[k], 1)
                    dve.wait_ge(s_setup, 1)
                    dve.wait_ge(ln_stat[k], c.b + 1)
                    for n in range(NC):
                        i = dve.bn_aggr(mv[k][:, n, :], st[:, n, :])
                    i.then_inc(ln_aggr[k], 1)
                    dve.wait_ge(ln_aggr[k], c.b + 1)
                    dve.tensor_scalar(ve[k][:, :], mv[k][:, :, 1], EPS, None, ALU.add).then_inc(ln_var[k], 1)
                return step

            def norm_out(k):
                def step(c):
                    dve.wait_ge(ln_rstd[k], c.b + 1)
                    dve.scalar_tensor_tensor(out=shift[k][:, :], in0=mv[k][:, :, 0], scalar=-1.0, in1=rstd[k][:, :],
                                             op0=ALU.mult, op1=ALU.mult).then_inc(ln_shift[k], 1)
                return step

            def lo(dst, src, hi):
                return dve.tensor_tensor(out=dst, in0=src, in1=hi.bitcast(fp32), op=ALU.subtract)

            def turn_in(c):
                dve.wait_ge(hT_hi, c.b + 1)
                lo(hT[1][:, :, :], psT[:, :, :], hT[0][:, :, :]).then_inc(hT_lo, 1)

            def m1(c):
                h, p = c.info
                dve.wait_ge(m1_hi, 2 * H * c.b + 2 * h + p + 1)
                ps = psA[c.pair]
                lo(whl[:, 2 * p:2 * p + 2, h, :], ps[:, :, 0:F], whx[:, 2 * p:2 * p + 2, h, 0:F]).then_inc(m1_lo, 1)
                dve.tensor_copy(fcol[:, 2 * p:2 * p + 2, h, :], ps[:, :, F:FA]).then_inc(m1_read, 1)

            def cols(q):
                h0, nh = heads_of(q)
                return (fcol2 if q == 2 else fcol)[:, :, h0:h0 + nh, :], (fs2 if q == 2 else fs)[:, :, h0:h0 + nh], nh

            def f2rows(c):
                q = c.info
                f, f_s, nh = cols(q)
                if q == 2:
                    dve.wait_ge(m2_read, 2 * (c.b + 1))
                else:
                    dve.wait_ge(m1_read, 2 * H * c.b + 4 * q + 4)
                dve.tensor_scalar(f_s, f[:, :, :, 1], SLOPE, None, ALU.mult).then_inc(c1_made[q], 1)
                dve.tensor_copy(c1[q][:, :, 0, 0:nh].bitcast(f32r), f[:, :, :, 1]).then_inc(c1_made[q], 1)
                dve.wait_ge(c1_made[q], 3 * c.b + 2)
                dve.tensor_tensor(out=c1[q][:, :, 1, 0:nh], in0=f[:, :, :, 1], in1=c1[q][:, :, 0, 0:nh],
                                  op=ALU.subtract).then_inc(c1_made[q], 1)

            def rowmax(c):
                q, hh = c.info
                nh = heads_of(q)[1]
                dve.wait_ge(f2_spread[q], nh * c.b + hh + 1)
                dve.memset(held[:, 0:1], 0.0)
                for n in range(NC):
                    if n == 2:
                        dve.wait_ge(max_made[q], NC * (nh * c.b + hh) + n)
                        dve.memset(held[:, 1:2], 0.0)
                    dve.tensor_tensor_reduce(out=junk[:, n % 2, :], in0=psT[:, hh, :], in1=mask[:, n, :], scale=1.0,
                                             scalar=-3.0e38, op0=ALU.add, op1=ALU.max,
                                             accum_out=gmax[q][:, n, hh:hh + 1]).then_inc(max_made[q], 1)
                dve.wait_ge(max_made[q], NC * (nh * c.b + hh + 1))
                dve.memset(held[:, 2:3], 0.0)

            def rowmath(c):
                q = c.info
                f, _, nh = cols(q)
                dve.wait_ge(max_made[q], nh * NC * (c.b + 1))
                z, m, ra, rb = (zrow[q][:, k, :, 0:nh] for k in range(4))
                f1 = f[:, :, :, 0]
                g = gmax[q][:, :, 0:nh]
                done = row_math[q]

                def after(k):
                    dve.wait_ge(done, 8 * c.b + k)

                dve.tensor_tensor(out=z, in0=f1, in1=g, op=ALU.add).then_inc(done, 1)
                after(1)
                dve.scalar_tensor_tensor(out=m, in0=z, scalar=SLOPE, in1=z, op0=ALU.mult, op1=ALU.max).then_inc(done, 1)
                after(2)
                dve.tensor_tensor(out=ra, in0=f1, in1=m, op=ALU.subtract).then_inc(done, 1)
                dve.scalar_tensor_tensor(out=rb, in0=f1, scalar=SLOPE, in1=m, op0=ALU.mult, op1=ALU.subtract).then_inc(done, 1)
                k = [c2[q][:, :, i, 0:nh] for i in range(4)]
                after(3)
                dve.tensor_copy(k[0].bitcast(f32r), ra).then_inc(done, 1)
                after(4)
                dve.tensor_copy(k[2].bitcast(f32r), rb).then_inc(done, 1)
                after(5)
                dve.tensor_tensor(out=k[1], in0=ra, in1=k[0], op=ALU.subtract).then_inc(done, 1)
                after(6)
                dve.tensor_tensor(out=k[3], in0=rb, in1=k[2], op=ALU.subtract).then_inc(done, 1)

            def args(c):
                f = fcol2[:, :, 0, 1] if c.h == BACK else fcol[:, :, c.h, 1]
                for j in range(NC):
                    dve.wait_ge(arg_lin, NC * c.unit + j + 1)
                    a = arg[:, c.buf, j, :]
                    dve.scalar_tensor_tensor(out=a, in0=psR[:, 0, c.u * HN:(c.u + 1) * HN], scalar=f[:, j:j + 1], in1=a,
                                             op0=ALU.add, op1=ALU.max).then_inc(arg_max, 1)

            def elu_in_(c):
                dve.wait_ge(att_done, c.unit + 1)
                dve.reciprocal(rec[:, c.buf, :], psA[c.pair][:, :, F]).then_inc(elu_rec, 1)

            def elu_neg_(c):
                dve.wait_ge(elu_x, c.unit + 1)
                wait(dve, elu_out, c.unit)
                dve.tensor_scalar(elu_ex[:, :, :], elu_in[:, c.buf, :, :], 0.0, None, ALU.min).then_inc(elu_neg, 1)

            def elu_out_(c):
                dve.wait_ge(elu_exp, c.unit + 1)
                if c.h == BACK:
                    dst = wk[:, 2 * c.u:2 * c.u + 2, :]
                else:
                    if not isinstance(c.b, int) or c.b > 0:
                        wait(dve, m2_turned, NC * (c.b - 1) + 2 * c.u + 2)
                    dst = hcat[:, 2 * c.u:2 * c.u + 2, c.h, :]
                dve.scalar_tensor_tensor(out=dst, in0=elu_ex[:, :, :], scalar=-1.0, in1=elu_in[:, c.buf, :, :],
                                         op0=ALU.add, op1=ALU.max).then_inc(elu_out, 1)

            hx_of_T = psT[:, :, :].rearrange("p a n -> p (a n)").rearrange("p (k n) -> p k n", k=OC)

            def turn2(c):
                dve.wait_ge(hx_hi, NC * c.b + c.info + 1)
                hx_ = turned[c.info % 2]
                lo(hx_[1][:, :, :], hx_of_T, hx_[0][:, :, :]).then_inc(hx_lo, 1)

            def mix2(c):
                dve.wait_ge(m2_hi, 2 * c.b + c.info + 1)
                ps, n = psA[c.pair], 2 * c.info
                lo(w2l[:, n:n + 2, :], ps[:, :, 0:F], w2x[:, n:n + 2, 0:F]).then_inc(m2_lo, 1)
                dve.tensor_copy(fcol2[:, n:n + 2, 0, :], ps[:, :, F:FA]).then_inc(m2_read, 1)

            def ffn2(c):
                dve.wait_ge(f2_done, c.b + 1)
                dve.tensor_tensor(out=wk[:, :, :], in0=psA[c.pair][:, :, :].rearrange("p a (c f) -> p (a c) f", c=2), in1=wk[:, :, :],
                                  op=ALU.add).then_inc(y_ready, 1)

            def x2(c):
                dve.wait_ge(y_gamma, c.b + 1)
                dve.wait_ge(x_beta, c.b + 1)
                dve.tensor_tensor(out=xb[:, :, :], in0=xb[:, :, :], in1=wk[:, :, :], op=ALU.add).then_inc(x2_ready, 1)

            def turn_gc(c):
                dve.wait_ge(h2_hi, c.b + 1)
                lo(h2T[1][:, :, :], psT[:, :, :], h2T[0][:, :, :]).then_inc(h2_lo, 1)

            def conv_in_(c):
                p, ps = c.info, psA[c.pair]
                dve.wait_ge(mj_hi, 2 * c.b + p + 1)
                lo(w2l[:, 2 * p:2 * p + 2, :], ps[:, :, F:2 * F], w2x[:, 2 * p:2 * p + 2, 0:F]).then_inc(mj_lo, 1)
                dve.wait_ge(ln_out["gc"], c.b + 1)
                for i in range(2):
                    n = 2 * p + i
                    r = dve.scalar_tensor_tensor(out=xb[:, n, :], in0=ps[:, i, 0:F], scalar=deg[:, n:n + 1], in1=xb[:, n, :],
                                                 op0=ALU.mult, op1=ALU.add)
                r.then_inc(conv_in_read, 1)

            def conv(c):
                dve.wait_ge(conv_done, c.b + 1)
                dve.wait_ge(conv_in_read, 2 * (c.b + 1))
                dve.tensor_tensor(out=xb[:, :, :], in0=psT[:, :, :].rearrange("p a (c f) -> p (a c) f", c=2), in1=xb[:, :, :],
                                  op=ALU.add).then_inc(res_ready, 1)

            run_all(dve, DVE_STEPS, {"norm_in": norm("in", xin, x_loaded, 16), "norm_in_out": norm_out("in"), "turn_in": turn_in, "m1": m1,
                                     "f2rows": f2rows, "rowmax": rowmax, "rowmath": rowmath, "args": args, "elu_in": elu_in_,
                                     "elu_neg": elu_neg_,
                                     "elu_out": elu_out_, "turn2": turn2, "mix2": mix2, "ffn2": ffn2,
                                     "norm_ff": norm("ff", wk, y_ready, 1), "norm_ff_out": norm_out("ff"), "x2": x2,
                                     "norm_gc": norm("gc", xb, x2_ready, 1), "norm_gc_out": norm_out("gc"),
                                     "turn_gc": turn_gc, "conv_in": conv_in_, "conv": conv},
                    after_first=setup_back)

        @block.tensor
        def _(pe):
            adj_f = arg[:, :, :, :].rearrange("p a c n -> p (a c n)").rearrange("p (c n) -> p c n", c=NC)
            pe.wait_ge(s_const, 3)
            pe.wait_ge(s_adj, 1 + NC)
            for n in range(NC):
                wait(pe, s_adj_out, n - 1)
                for j in range(NC):
                    pe.transpose(psT[:, n % 2, j * P:(j + 1) * P], adj_f[:, n, j * P:(j + 1) * P], ident[:, :])
                    i = pe.transpose(psA[n % 2][:, 0, j * P // 2:(j + 1) * P // 2].bitcast(bf16), mask[:, n, j * P:(j + 1) * P], identb)
                i.then_inc(s_adj_turned, 1)
            pe.wait_ge(ld[LD_GC], 16)
            w_gc = xb[:, :, :].rearrange("p (a c) f -> p a (c f)", a=2)
            for k in range(KC):
                for side in range(2):
                    for o in range(KC):
                        i = pe.transpose(psR[:, k, side * F + o * P:side * F + (o + 1) * P],
                                         w_gc[:, o, side * F + k * P:side * F + (k + 1) * P], ident[:, :])
            i.then_inc(s_gc_turned, 1)
            for l in (LD_W1, LD_W2):
                pe.wait_ge(ld[l], 16)
            pe.wait_ge(s_setup, 1)

            lent = {}

            def take(ps, c):
                if ps in lent:
                    s, at, late = lent[ps]
                    wait(pe, s, at(c.r + c.late - late))

            def lend(ps, c, s, at):
                lent[ps] = (s, at, c.late)

            def take_psT(c):
                take("T0", c)
                if lent.get("T1") != lent.get("T0"):
                    take("T1", c)

            def lend_psT(c, s, at):
                lend("T0", c, s, at)
                lent["T1"] = lent["T0"]

            def at_trip_end():
                for ps, (s, at, late) in lent.items():
                    lent[ps] = (s, at, late + 1)

            def product(out, steps, wide=None, also=None):
                n = 3 * len(steps)
                k = 0
                for lh, ll, rh, rl in steps:
                    for a, b_, o in ((lh, rh, wide if wide is not None else out), (ll, rh, wide if wide is not None else out), (lh, rl, out)):
                        i = pe.matmul(o, a, b_, start=(k == 0), stop=(k == n - 1))
                        k += 1
                        if also and k == 1:
                            pe.matmul(*also, start=False, stop=False)
                return i

            def wait_setup_back(c):
                if isinstance(c.b, int) and c.b == 0 and c.info == 0:
                    pe.wait_ge(s_setup_back, 1)

            def turn_in(c):
                pe.wait_ge(ln_out["in"], c.b + 1)
                take_psT(c)
                for k in range(KC):
                    for n in range(NC):
                        i = pe.transpose(psT[:, k, n * P:(n + 1) * P], xin[:, n, k * P:(k + 1) * P], ident[:, :])
                i.then_inc(h_turned, 1)
                lend_psT(c, hT_lo, lambda r: r + 2)

            def m1(c):
                h, p = c.info
                pe.wait_ge(hT_lo, c.b + 1)
                take(c.pair, c)
                for i in range(2):
                    n = 2 * p + i
                    r = product(psA[c.pair][:, i, 0:FA],
                                [(hT[0][:, k, n * P:(n + 1) * P], hT[1][:, k, n * P:(n + 1) * P], wh[0][:, k, h, :], wh[1][:, k, h, :])
                                 for k in range(KC)])
                r.then_inc(m1_done, 1)
                off = 1 if h < 2 else 0
                lend(c.pair, c, m1_read, lambda r: 2 * H * (r + off) + 2 * h + p + 1)

            def f2rows(c):
                q = c.info
                pe.wait_ge(c1_made[q], 3 * (c.b + 1))
                take("T0", c)
                for n in range(NC):
                    i = pe.transpose(psT[0:4, 0, n * P:(n + 1) * P], c1[q][:, n, :, :].rearrange("p a h -> p (a h)"), ident[:, :])
                i.then_inc(c1_turned[q], 1)
                off = (1, 0, -1)[q]
                lend("T0", c, f2row_made[q], lambda r: r + off + 1)

            def rowmax(c):
                q, hh = c.info
                nh, off = heads_of(q)[1], (1, 0, -1)[q]
                pe.wait_ge(f2row_made[q], c.b + 1)
                take(f"T{hh}", c)
                pe.matmul(psT[:, hh, :], pick[:, hh, :], f2row[:, :], start=True, stop=True).then_inc(f2_spread[q], 1)
                lend(f"T{hh}", c, max_made[q], lambda r: NC * (nh * (r + off) + hh + 1))

            def rows(c):
                q = c.info
                pe.wait_ge(row_math[q], 8 * (c.b + 1))
                take("T1", c)
                for n in range(NC):
                    i = pe.transpose(psT[0:8, 1, n * P:(n + 1) * P], c2[q][:, n, :, :].rearrange("p a h -> p (a h)"), ident[:, :])
                i.then_inc(c2_turned[q], 1)
                off = (1, 0, -1)[q]
                lend("T1", c, rrow_made[q], lambda r: r + off + 1)

            def spread_(c):
                q, hh = (2, 0) if c.h == BACK else (c.h // 2, c.h % 2)
                pe.wait_ge(rrow_made[q], c.b + 1)
                wait(pe, arg_max, NC * c.unit)
                for w in range(2):
                    pe.matmul(psR[:, w, :], pick[:, 2 * w + hh, :], rrow[q][:, :], start=True, stop=True).then_inc(spread, 1)

            def attend(c):
                pe.wait_ge(prob_lo, c.unit + 1)
                if c.h == BACK:
                    pe.wait_ge(m2_read, 2 * (c.b + 1))
                    hi, low = (lambda j: w2x[:, j, :]), (lambda j: w2l[:, j, :])
                else:
                    pe.wait_ge(m1_read, 2 * H * c.b + 2 * c.h + 2)
                    hi, low = (lambda j: whx[:, j, c.h, :]), (lambda j: whl[:, j, c.h, :])
                take(c.pair, c)
                for n in range(2):
                    r = product(psA[c.pair][:, n, 0:F],
                                [(prob[0][:, c.buf, j, n * P:(n + 1) * P], prob[1][:, c.buf, j, n * P:(n + 1) * P], hi(j), low(j))
                                 for j in range(NC)], wide=psA[c.pair][:, n, 0:FA])
                r.then_inc(att_done, 1)
                lend(c.pair, c, elu_x, lambda r: unit_number(r, c.info) + 1)

            def turn2(c):
                pe.wait_ge(elu_out, c.before)
                take_psT(c)
                for k in range(OC):
                    i = pe.transpose(psT[:, k // 4, (k % 4) * P:(k % 4 + 1) * P], hcat[:, c.info, k // KC, (k % KC) * P:(k % KC + 1) * P],
                                     ident[:, :])
                i.then_inc(m2_turned, 1)
                n = c.info
                lend_psT(c, hx_lo, lambda r: NC * (r - 1) + n + 1)

            def mix2(c):
                wait_setup_back(c)
                pe.wait_ge(hx_lo, NC * c.b + c.info + 1)
                hx_ = turned[c.info % 2]
                if c.info % 2 == 0:
                    take(c.pair, c)
                product(psA[c.pair][:, c.info % 2, 0:FA],
                        [(hx_[0][:, k, :], hx_[1][:, k, :], wo[0][:, k, :], wo[1][:, k, :]) for k in range(OC)]).then_inc(m2_done, 1)
                n = c.info
                lend(c.pair, c, m2_read, lambda r: 2 * (r - 1) + n // 2 + 1)

            def turn_out(c):
                pe.wait_ge(elu_out, unit_number(c.r, 5) + 1)
                take_psT(c)
                for k in range(KC):
                    for n in range(NC):
                        i = pe.transpose(psT[:, k, n * P:(n + 1) * P], wk[:, n, k * P:(k + 1) * P], ident[:, :])
                i.then_inc(o_turned, 1)
                lend_psT(c, oT_ready, lambda r: r)

            outT = ff[:, 0, :, :].rearrange("p c f -> p (c f)").rearrange("p (k n) -> p k n", k=KC)
            midT = ff[:, 1, :, :].rearrange("p c f -> p (c f)").rearrange("p (k n) -> p k n", k=KC)

            def ffn1(c):
                pe.wait_ge(oT_ready, c.b + 1)
                take(c.pair, c)
                for o in range(KC):
                    for k in range(KC):
                        i = pe.matmul(psA[c.pair][:, o, :], w1_sb[:, k, o * P:(o + 1) * P], outT[:, k, :], start=(k == 0), stop=(k == KC - 1))
                    i.then_inc(f1_done, 1)
                lend(c.pair, c, f1_read, lambda r: KC * r)

            def ffn2(c):
                pe.wait_ge(f1_read, KC * (c.b + 1))
                take(c.pair, c)
                for n in range(NC):
                    y = psA[c.pair][:, n // 2, (n % 2) * F:(n % 2 + 1) * F]
                    pe.matmul(y, pick[:, 1, :], brow[:, :], start=True, stop=False)
                    for k in range(KC):
                        i = pe.matmul(y, midT[:, k, n * P:(n + 1) * P], w2_sb[:, k, :], start=False, stop=(k == KC - 1))
                i.then_inc(f2_done, 1)
                lend(c.pair, c, y_ready, lambda r: r)

            def turn_gc(c):
                pe.wait_ge(ln_out["gc"], c.b + 1)
                take_psT(c)
                for k in range(KC):
                    for n in range(NC):
                        i = pe.transpose(psT[:, k, n * P:(n + 1) * P], ff[:, 1, n, k * P:(k + 1) * P], ident[:, :])
                i.then_inc(h2_turned, 1)
                lend_psT(c, h2_lo, lambda r: r)

            def conv_in_(c):
                pe.wait_ge(h2_lo, c.b + 1)
                take(c.pair, c)
                for i in range(2):
                    n = 2 * c.info + i
                    r = product(psA[c.pair][:, i, :],
                                [(h2T[0][:, k, n * P:(n + 1) * P], h2T[1][:, k, n * P:(n + 1) * P], wg[0][:, k, :], wg[1][:, k, :]) for k in range(KC)],
                                also=(psA[c.pair][:, i, 0:F], pick[:, 0, :], brow[:, :]))
                r.then_inc(conv_in, 1)
                p = c.info
                lend(c.pair, c, conv_in_read, lambda r: 2 * (r - 1) + p + 1)

            def conv(c):
                pe.wait_ge(mj_lo, 2 * (c.b + 1))
                take_psT(c)
                for n in range(NC):
                    for j in range(NC):
                        for s, mj in enumerate((w2x[:, j, 0:F], w2l[:, j, :])):
                            i = pe.matmul(psT[:, n // 2, (n % 2) * F:(n % 2 + 1) * F], adjT[:, j, n * P:(n + 1) * P], mj,
                                          start=(j == 0 and s == 0), stop=(j == NC - 1 and s == 1))
                i.then_inc(conv_done, 1)
                lend_psT(c, res_ready, lambda r: r)

            run_all(pe, PE_STEPS, {"turn_in": turn_in, "m1": m1, "f2rows": f2rows, "rowmax": rowmax, "rows": rows, "spread": spread_,
                         "attend": attend, "turn2": turn2, "mix2": mix2, "turn_out": turn_out, "ffn1": ffn1, "ffn2": ffn2,
                         "turn_gc": turn_gc, "conv_in": conv_in_, "conv": conv}, at_trip_end)


_INS = ["x", "adj", "L0_gnn_W_heads", "L0_gnn_a_heads", "L0_gnn_W_out", "L0_gnn_a_out", "L0_gnn_w1", "L0_gnn_b1",
        "L0_gnn_w2", "L0_gnn_b2", "L0_gnn_ln_gamma", "L0_gnn_ln_beta", "L1_gnn_W", "L1_gnn_b"]


def kernel(**inputs):
    import numpy as _np
    import concourse.bacc as _bacc
    from concourse import mybir as _mybir
    from concourse.bass_utils import run_bass_kernel_spmd as _run

    nc = _bacc.Bacc("TRN2", target_bir_lowering=False, num_devices=1)
    arrays, args = {}, []
    for name in _INS:
        a = _np.ascontiguousarray(inputs[name])
        arrays[f"in_{name}"] = a
        args.append(nc.dram_tensor(f"in_{name}", a.shape, _mybir.dt.from_np(a.dtype), kind="ExternalInput").ap())
    shape = arrays["in_x"].shape
    out = nc.dram_tensor("out_x", shape, _mybir.dt.float32, kind="ExternalOutput").ap()
    gnn_kernel(nc, *args, out)
    r = _run(nc, [arrays], core_ids=[0])
    return r.results[0]["out_x"]
```
